# Optimizing a Trainium2 kernel written in Bass

```python
import numpy as np
import jax
import jax.numpy as jnp

def _softmax(x, axis=-1):
    return jax.nn.softmax(x, axis=axis)

def _gelu(x):
    return jax.nn.gelu(x, approximate=True)

def _silu(x):
    return jax.nn.silu(x)

def _sigmoid(x):
    return jax.nn.sigmoid(x)

def _layernorm(x, axis=-1, eps=1e-05):
    m = jnp.mean(x, axis=axis, keepdims=True)
    v = jnp.var(x, axis=axis, keepdims=True)
    return (x - m) / jnp.sqrt(v + eps)

def _scatter_add(tgt, idx, src, axis=0):
    return tgt.at[idx].add(src)

def _segment_sum(src, seg, n):
    return jax.ops.segment_sum(src, seg, n)
kernel_name = 'mk_flamingo_gated_d1_seqx_r2_535196'

def setup_inputs(seed: int=0):
    np.random.seed(seed)
    _w = jnp.asarray

    def _rec_inputs():
        import jax
        import jax.numpy as jnp
        _rk = jax.random.key(seed)
        x = -0.0002928 + 1 * jax.random.normal(jax.random.fold_in(_rk, 1), (16, 512, 512), jnp.float32)
        _lenS = 512 - jax.random.randint(jax.random.fold_in(_rk, 7), (16,), 0, max(1, 512 // 4) + 1, jnp.int32)
        _lenS2 = 77 - jax.random.randint(jax.random.fold_in(_rk, 8), (16,), 0, max(1, 77 // 4) + 1, jnp.int32)
        _ctx_1024P = jax.random.normal(jax.random.fold_in(_rk, 11), (16, 16, 512), jnp.float32)
        _ctx_1024c = jax.random.dirichlet(jax.random.fold_in(_rk, 511), 0.3 * jnp.ones((16,), jnp.float32), (16, 77))
        _ctx_1024t = jnp.einsum('bsk,bkd->bsd', _ctx_1024c, _ctx_1024P)
        _ctx_1024t = _ctx_1024t * jax.lax.rsqrt(jnp.mean(jnp.square(_ctx_1024t)) + 1e-12) * 0.953939
        ctx_1024 = -1.39393e-06 + 0.999914 * (_ctx_1024t + 0.3 * jax.random.normal(jax.random.fold_in(_rk, 611), (16, 77, 512), jnp.float32))
        _g = jax.random.normal(jax.random.fold_in(_rk, 9001), (2, 1), jnp.float32)
        _g = jnp.sign(_g) * jnp.maximum(jnp.abs(_g), 1.0) + (_g == 0) * 1.0
        g_xattn = _g[0]
        g_ffn = _g[1]
        return (x, ctx_1024, g_xattn, g_ffn)
    x, ctx_1024, g_xattn, g_ffn = _rec_inputs()

    def _L0_xattn_setup():
        import jax, jax.numpy as jnp
        import numpy as np
        DIM = 512
        N_HEADS = 16
        HEAD_DIM = DIM // N_HEADS
        B, N, M = (2, 1024, 1024)
        key = jax.random.key(seed)
        ks = jax.random.split(key, 10)
        s = 1.0 / np.sqrt(DIM)
        return {'x1': jax.random.normal(ks[0], (B, N, DIM), dtype=jnp.float32), 'x2': jax.random.normal(ks[1], (B, M, DIM), dtype=jnp.float32), 'Wq': jax.random.normal(ks[2], (DIM, DIM), dtype=jnp.float32) * s, 'bq': jnp.zeros((DIM,), dtype=jnp.float32), 'Wk': jax.random.normal(ks[3], (DIM, DIM), dtype=jnp.float32) * s, 'bk': jnp.zeros((DIM,), dtype=jnp.float32), 'Wv': jax.random.normal(ks[4], (DIM, DIM), dtype=jnp.float32) * s, 'bv': jnp.zeros((DIM,), dtype=jnp.float32), 'Wo': jax.random.normal(ks[5], (DIM, DIM), dtype=jnp.float32) * s, 'bo': jnp.zeros((DIM,), dtype=jnp.float32)}
    _L0_xattn_all = _L0_xattn_setup()
    _L0_xattn_in = {k: v for k, v in _L0_xattn_all.items() if k in ('Wq', 'bq', 'Wk', 'bk', 'Wv', 'bv', 'Wo', 'bo')}
    del _L0_xattn_all

    def _L0_ffn_setup():
        import jax, jax.numpy as jnp
        import numpy as np
        B, S, D_MODEL, D_FF = (4, 1024, 512, 2048)

        def _quantum_transform(hidden, theta, w_real, w_imag):
            imag = w_imag * jnp.sin(theta + hidden * 0.1)
            quantum_phase = jnp.cos(theta) * w_real + jnp.sin(theta) * w_imag
            return hidden + quantum_phase * imag * 0.1
        key = jax.random.key(seed)
        ks = jax.random.split(key, 8)
        return {'x': jax.random.normal(ks[0], (B, S, D_MODEL), dtype=jnp.float32), 'W1': jax.random.normal(ks[1], (D_MODEL, D_FF), dtype=jnp.float32) * (1.0 / np.sqrt(D_MODEL)), 'b1': jnp.zeros((D_FF,), dtype=jnp.float32), 'quantum_phases': jax.random.normal(ks[2], (D_FF,), dtype=jnp.float32) * (2.0 * np.pi), 'quantum_weights_real': jax.random.normal(ks[3], (D_FF,), dtype=jnp.float32) * 0.1, 'quantum_weights_imag': jax.random.normal(ks[4], (D_FF,), dtype=jnp.float32) * 0.1, 'W2': jax.random.normal(ks[5], (D_FF, D_MODEL), dtype=jnp.float32) * (1.0 / np.sqrt(D_FF)), 'b2': jnp.zeros((D_MODEL,), dtype=jnp.float32)}
    _L0_ffn_all = _L0_ffn_setup()
    _L0_ffn_in = {k: v for k, v in _L0_ffn_all.items() if k in ('W1', 'b1', 'quantum_phases', 'quantum_weights_real', 'quantum_weights_imag', 'W2', 'b2')}
    del _L0_ffn_all
    return {'x': x, 'ctx_1024': ctx_1024, 'g_xattn': g_xattn, 'g_ffn': g_ffn, 'L0_xattn_Wq': _L0_xattn_in['Wq'], 'L0_xattn_bq': _L0_xattn_in['bq'], 'L0_xattn_Wk': _L0_xattn_in['Wk'], 'L0_xattn_bk': _L0_xattn_in['bk'], 'L0_xattn_Wv': _L0_xattn_in['Wv'], 'L0_xattn_bv': _L0_xattn_in['bv'], 'L0_xattn_Wo': _L0_xattn_in['Wo'], 'L0_xattn_bo': _L0_xattn_in['bo'], 'L0_ffn_W1': _L0_ffn_in['W1'], 'L0_ffn_b1': _L0_ffn_in['b1'], 'L0_ffn_quantum_phases': _L0_ffn_in['quantum_phases'], 'L0_ffn_quantum_weights_real': _L0_ffn_in['quantum_weights_real'], 'L0_ffn_quantum_weights_imag': _L0_ffn_in['quantum_weights_imag'], 'L0_ffn_W2': _L0_ffn_in['W2'], 'L0_ffn_b2': _L0_ffn_in['b2']}

def reference(x, ctx_1024, g_xattn, g_ffn, L0_xattn_Wq, L0_xattn_bq, L0_xattn_Wk, L0_xattn_bk, L0_xattn_Wv, L0_xattn_bv, L0_xattn_Wo, L0_xattn_bo, L0_ffn_W1, L0_ffn_b1, L0_ffn_quantum_phases, L0_ffn_quantum_weights_real, L0_ffn_quantum_weights_imag, L0_ffn_W2, L0_ffn_b2):
    import jax
    import jax.numpy as jnp

    def _L0_xattn_ref(x1, x2, Wq, bq, Wk, bk, Wv, bv, Wo, bo):
        import jax, jax.numpy as jnp
        import numpy as np
        DIM = 512
        N_HEADS = 16
        HEAD_DIM = DIM // N_HEADS
        B, N, M = (2, 1024, 1024)
        b, n, _ = x1.shape
        m = x2.shape[1]
        q = x1 @ Wq.T + bq
        k = x2 @ Wk.T + bk
        v = x2 @ Wv.T + bv
        q = q.reshape(b, n, N_HEADS, HEAD_DIM).transpose(0, 2, 1, 3)
        k = k.reshape(b, m, N_HEADS, HEAD_DIM).transpose(0, 2, 1, 3)
        v = v.reshape(b, m, N_HEADS, HEAD_DIM).transpose(0, 2, 1, 3)
        scale = 1.0 / jnp.sqrt(jnp.asarray(HEAD_DIM, dtype=q.dtype))
        scores = jnp.einsum('bhnd,bhmd->bhnm', q, k) * scale
        attn = jax.nn.softmax(scores, axis=-1)
        o = jnp.einsum('bhnm,bhmd->bhnd', attn, v)
        o = o.transpose(0, 2, 1, 3).reshape(b, n, DIM)
        return o @ Wo.T + bo

    def _L0_ffn_ref(x, W1, b1, quantum_phases, quantum_weights_real, quantum_weights_imag, W2, b2):
        import jax, jax.numpy as jnp
        import numpy as np
        B, S, D_MODEL, D_FF = (4, 1024, 512, 2048)

        def _quantum_transform(hidden, theta, w_real, w_imag):
            imag = w_imag * jnp.sin(theta + hidden * 0.1)
            quantum_phase = jnp.cos(theta) * w_real + jnp.sin(theta) * w_imag
            return hidden + quantum_phase * imag * 0.1
        hidden = jnp.einsum('bsd,df->bsf', x, W1) + b1
        q = _quantum_transform(hidden, quantum_phases, quantum_weights_real, quantum_weights_imag)
        act = jax.nn.relu(q)
        return jnp.einsum('bsf,fd->bsd', act, W2) + b2
    x = x + jnp.tanh(g_xattn[0]) * _L0_xattn_ref(_layernorm(x, axis=-1), ctx_1024, L0_xattn_Wq, L0_xattn_bq, L0_xattn_Wk, L0_xattn_bk, L0_xattn_Wv, L0_xattn_bv, L0_xattn_Wo, L0_xattn_bo)
    x = x + jnp.tanh(g_ffn[0]) * _L0_ffn_ref(_layernorm(x, axis=-1), L0_ffn_W1, L0_ffn_b1, L0_ffn_quantum_phases, L0_ffn_quantum_weights_real, L0_ffn_quantum_weights_imag, L0_ffn_W2, L0_ffn_b2)
    return x

_drawn_inputs = setup_inputs


def setup_inputs(seed=0):
    import zlib

    import numpy as np

    out = dict(_drawn_inputs(seed))
    spreads = {'L0_xattn_bq': (0.0, 0.499),
     'L0_xattn_bk': (0.0, 2.0),
     'L0_xattn_bv': (0.0, 0.1),
     'L0_xattn_bo': (0.0, 0.1),
     'L0_ffn_b1': (0.0, 0.1),
     'L0_ffn_b2': (0.0, 0.1)}
    factors = {'L0_ffn_quantum_phases': 8.0,
     'L0_ffn_quantum_weights_real': 41.783,
     'L0_ffn_quantum_weights_imag': 8.0}
    for name, (base, spread) in spreads.items():
        noise = np.random.default_rng([zlib.crc32(name.encode()), seed]).standard_normal(out[name].shape)
        drawn = base * np.exp(spread * noise) if base else spread * noise
        out[name] = jnp.asarray(drawn.astype(out[name].dtype))
    for name, factor in factors.items():
        out[name] = (out[name] * factor).astype(out[name].dtype)
    return out
```

```python
from contextlib import ExitStack

import concourse.bass as bass
from concourse import mybir

F32 = mybir.dt.float32
F32R = mybir.dt.float32r
ALU = mybir.AluOpType
ACT = mybir.ActivationFunctionType
AX_X = mybir.AxisListType.X

P = 128
HEADS = 16
EPS = 1e-5
TWO_PI = 6.283185307179586
TWO_PI_PARTS = (6.28125, 0.00193405151367187500, TWO_PI - 6.28125 - 0.00193405151367187500)
TWO_PI_BELOW = 6.2831850051879883
ROUND_MAGIC = 12582912.0

PASSES = ((0, 0), (0, 1), (1, 0))


def matmul3(pe, out, stationary, moving, first, last):
    for n, (s, m) in enumerate(PASSES):
        mm = pe.matmul(out, stationary(s), moving(m), start=first and n == 0,
                       stop=last and n == len(PASSES) - 1)
    return mm


class Count:

    def __init__(self, done, parity):
        self.done, self.parity, self.uses = done, parity, 0

    def next(self):
        self.uses += 1
        return self.done + self.uses, (self.parity + self.uses - 1) % 2


def gated_attention_ffn_kernel(nc, x, ctx_in, g_xattn, g_ffn, wq, bq, wk, bk, wv, bv, wo, bo,
                               w1, b1, phases, w_real, w_imag, w2, b2, out):
    B, N, D = x.shape
    M = ctx_in.shape[1]
    F = w1.shape[1]
    DH = D // HEADS
    KT = D // P
    NT = N // P
    FT = F // P
    G = D // P
    HG = P // DH
    GC = HG * M
    NC = -(-GC // P)
    HALF = NT // 2
    UR = HALF * HG
    CB = 4
    ROUNDS = B // CB
    SCALE = float(DH) ** -0.5
    NVEC = 4 * FT + 2 * G
    assert N == 512 and D == 512 and G == KT == NT == 4 and B % CB == 0 and NC == 3 and FT == 16

    x1 = nc.dram_tensor("x1_scratch", [B, N, D], F32).ap()
    k_parts = nc.dram_tensor("k_scratch", [B, G, P, 2, M], F32).ap()
    v_parts = nc.dram_tensor("v_scratch", [B, M, 2, D], F32).ap()

    x_tiles = x.rearrange("b (t p) d -> b p t d", p=P)
    x1_tiles = x1.rearrange("b (t p) d -> b p t d", p=P)
    out_tiles = out.rearrange("b (t p) d -> b p t d", p=P)

    with ExitStack() as whole:
        def sb(stack, name, shape, dt=F32):
            return stack.enter_context(nc.sbuf_tensor(name, shape, dt))

        def sem(stack, name):
            return stack.enter_context(nc.semaphore(name))

        pair_bank = [whole.enter_context(nc.psum_tensor(f"pair_bank{i}", [P, 2, 512], F32)) for i in range(2)]
        t_bank = [whole.enter_context(nc.psum_tensor(f"t_bank{i}", [P, 512], F32)) for i in range(2)]
        m_bank = [whole.enter_context(nc.psum_tensor(f"m_bank{i}", [P, 512], F32)) for i in range(2)]

        ident = sb(whole, "ident", [P, P])
        minus_half = sb(whole, "minus_half", [P, NT])
        tanh_g = sb(whole, "tanh_g", [P, 2])
        columns = sb(whole, "columns", [P, NVEC])
        b1_col = columns[:, 0:FT]
        phase_col = columns[:, FT:2 * FT]
        real_col = columns[:, 2 * FT:3 * FT]
        imag_col = columns[:, 3 * FT:4 * FT]
        bq_col = columns[:, 4 * FT:4 * FT + G]
        bk_col = columns[:, 4 * FT + G:NVEC]

        def setup(att, wqT, woT):
            st = ExitStack()
            with st:
                wkT = [sb(st, f"wkT{i}", [P, KT, D], F32R) for i in range(2)]
                wvT = [sb(st, f"wvT{i}", [P, KT, D], F32R) for i in range(2)]
                w_raw = [sb(st, f"w_raw{i}", [P, KT, D]) for i in range(4)]
                vector_rows = sb(st, "vector_rows", [NVEC, P])
                g_raw = sb(st, "g_raw", [P, 2])
                bv_rows = sb(st, "bv_rows", [M, D])
                ctx_raw = sb(st, "ctx_raw", [M, CB, D])
                ctxT = [sb(st, f"ctxT{i}", [P, KT, CB * M], F32R) for i in range(2)]
                kT = sb(st, "kT", [P, G, 2, CB * M], F32R)
                v_sum = [sb(st, f"v_sum{i}", [M, D]) for i in range(2)]
                v_split = [sb(st, f"v_split{i}", [M, 2, D], F32R) for i in range(2)]

                weights_loaded = [sem(st, f"weights_loaded{i}") for i in range(4)]
                vectors_loaded = sem(st, "vectors_loaded")
                bv_loaded = sem(st, "bv_loaded")
                ctx_loaded = sem(st, "ctx_loaded")
                zeroed = sem(st, "zeroed")
                ident_ready = sem(st, "ident_ready")
                vectors_ready = sem(st, "vectors_ready")
                t_full = sem(st, "t_full_s")
                t_hi = sem(st, "t_hi_s")
                t_split = sem(st, "t_split_s")
                m_full = sem(st, "m_full_s")
                m_hi = sem(st, "m_hi_s")
                m_split = sem(st, "m_split_s")
                v_summed = sem(st, "v_summed")
                k_stored = sem(st, "k_stored")
                v_stored = [sem(st, f"v_stored{i}") for i in range(2)]

                splits = (wqT, woT, wkT, wvT)
                T_HEAD = 1 + len(splits) * KT
                M_ROUND = G + CB

                block = st.enter_context(nc.Block())

                @block.sync
                def _(sp):
                    row = 0
                    for vec in (b1, phases, w_real, w_imag, bq, bk):
                        rows = vec.rearrange("(t p) -> t p", p=P)
                        sp.dma_start(vector_rows[row:row + rows.shape[0], :], rows).then_inc(vectors_loaded, 16)
                        row += rows.shape[0]
                    for i, g in enumerate((g_xattn, g_ffn)):
                        sp.dma_start(g_raw[:, i:i + 1], g.rearrange("(a b) -> a b", b=1).to_broadcast([P, 1]))\
                          .then_inc(vectors_loaded, 16)
                    for i, w in enumerate((wq, wo, wk, wv)):
                        sp.dma_start(w_raw[i][:, :, :], w.rearrange("(t p) k -> p t k", p=P))\
                          .then_inc(weights_loaded[i], 16)
                    sp.dma_start(bv_rows[:, :], bv.rearrange("(a d) -> a d", a=1).to_broadcast([M, D]))\
                      .then_inc(bv_loaded, 16)

                    def load_context(r):
                        sp.dma_start(ctx_raw[:, :, :], ctx_in[bass.ds(CB * r, CB)].rearrange("b m d -> m b d"))\
                          .then_inc(ctx_loaded, 16)

                    def round_of(r, last):
                        if not last:
                            sp.wait_ge(t_full, T_HEAD + KT * (r + 1))
                            load_context(r + 1)
                        for g in range(G):
                            sp.wait_ge(m_split, M_ROUND * r + g + 1)
                            for j in range(CB):
                                sp.dma_start(k_parts[CB * r + j, g], kT[:, g, :, j * M:(j + 1) * M].bitcast(F32))\
                                  .then_inc(k_stored, 16)
                        for j in range(CB):
                            sp.wait_ge(m_split, M_ROUND * r + G + j + 1)
                            sp.dma_start(v_parts[CB * r + j], v_split[j % 2][:, :, :].bitcast(F32))\
                              .then_inc(v_stored[j % 2], 16)

                    load_context(0)
                    with sp.Fori(0, ROUNDS - 1) as r:
                        round_of(r, False)
                    round_of(ROUNDS - 1, True)
                    sp.wait_ge(k_stored, 16 * CB * G * ROUNDS)
                    for i in range(2):
                        sp.wait_ge(v_stored[i], 16 * (CB // 2) * ROUNDS)

                @block.gpsimd
                def _(pool):
                    pool.memset(minus_half[:, :], -0.5)
                    pool.memset(ident[:, :], 0.0).then_inc(zeroed, 1)
                    pool.wait_ge(zeroed, 1)
                    pool.affine_select(out=ident[:, :], in_=ident[:, :], compare_op=ALU.not_equal, fill=1.0,
                                       base=0, pattern=[[-1, P]], channel_multiplier=1).then_inc(ident_ready, 1)

                @block.tensor
                def _(pe):
                    pe.wait_ge(ident_ready, 1)
                    pe.wait_ge(vectors_loaded, 16 * 8)
                    pe.transpose(t_bank[0][:, 0:NVEC], vector_rows[:, :], ident[0:NVEC, 0:NVEC]).then_inc(t_full, 1)
                    t = 1
                    for i in range(len(splits)):
                        pe.wait_ge(weights_loaded[i], 16)
                        for kt in range(KT):
                            if t == 2:
                                pe.wait_ge(vectors_ready, 1)
                            if t > 2:
                                pe.wait_ge(t_split, t - 2)
                            for ot in range(KT):
                                tr = pe.transpose(t_bank[t % 2][:, ot * P:(ot + 1) * P],
                                                  w_raw[i][:, ot, kt * P:(kt + 1) * P], ident[:, :])
                            tr.then_inc(t_full, 1)
                            t += 1

                    def round_of(r, first):
                        pe.wait_ge(ctx_loaded, 16 * (r + 1))
                        for kt in range(KT):
                            pe.wait_ge(t_split, T_HEAD - 2 + KT * r + kt)
                            for j in range(CB):
                                tr = pe.transpose(t_bank[(T_HEAD + kt) % 2][:, j * M:(j + 1) * M],
                                                  ctx_raw[:, j, kt * P:(kt + 1) * P], ident[0:M, 0:M])
                            tr.then_inc(t_full, 1)
                        pe.wait_ge(t_split, T_HEAD - 1 + KT * (r + 1))
                        for g in range(G):
                            if not (first and g < 2):
                                pe.wait_ge(m_split, M_ROUND * r + g - 1)
                            for kt in range(KT):
                                mm = matmul3(pe, m_bank[g % 2][:, 0:CB * M],
                                             lambda p: wkT[p][:, kt, g * P:(g + 1) * P],
                                             lambda p: ctxT[p][:, kt, :], kt == 0, kt == KT - 1)
                            mm.then_inc(m_full, 1)
                        for j in range(CB):
                            pe.wait_ge(m_split, M_ROUND * r + G + j - 1)
                            for kt in range(KT):
                                mm = matmul3(pe, m_bank[(G + j) % 2][0:M, :],
                                             lambda p: ctxT[p][:, kt, j * M:(j + 1) * M],
                                             lambda p: wvT[p][:, kt, :], kt == 0, kt == KT - 1)
                            mm.then_inc(m_full, 1)

                    round_of(0, True)
                    with pe.Fori(1, ROUNDS) as r:
                        round_of(r, False)

                @block.scalar
                def _(act):
                    act.wait_ge(vectors_loaded, 16 * 8)
                    act.activation(tanh_g[:, :], g_raw[:, :], ACT.Tanh)
                    for i, parts in enumerate(splits):
                        for kt in range(KT):
                            t = 1 + KT * i + kt
                            act.wait_ge(t_full, t + 1)
                            act.activation(parts[0][:, kt, :], t_bank[t % 2][:, :], ACT.Copy).then_inc(t_hi, 1)
                    act.wait_ge(vectors_ready, 1)

                    def round_of(r, first):
                        for kt in range(KT):
                            act.wait_ge(t_full, T_HEAD + KT * r + kt + 1)
                            act.activation(ctxT[0][:, kt, :], t_bank[(T_HEAD + kt) % 2][:, 0:CB * M], ACT.Copy)\
                               .then_inc(t_hi, 1)
                        for g in range(G):
                            act.wait_ge(m_full, M_ROUND * r + g + 1)
                            if g == 0 and not first:
                                act.wait_ge(k_stored, 16 * CB * G * r)
                            act.activation(kT[:, g, 0, :], m_bank[g % 2][:, 0:CB * M], ACT.Identity,
                                           bias=bk_col[:, g:g + 1]).then_inc(m_hi, 1)
                        for j in range(CB):
                            act.wait_ge(v_summed, CB * r + j + 1)
                            if not (first and j < 2):
                                act.wait_ge(v_stored[j % 2], 16 * ((CB // 2) * r + j // 2))
                            act.activation(v_split[j % 2][:, 0, :], v_sum[j % 2][:, :], ACT.Copy).then_inc(m_hi, 1)

                    round_of(0, True)
                    with act.Fori(1, ROUNDS) as r:
                        round_of(r, False)

                @block.vector
                def _(dve):
                    dve.wait_ge(t_full, 1)
                    dve.tensor_copy(columns[:, :], t_bank[0][:, 0:NVEC]).then_inc(vectors_ready, 1)
                    for i, parts in enumerate(splits):
                        for kt in range(KT):
                            t = 1 + KT * i + kt
                            dve.wait_ge(t_hi, t)
                            dve.tensor_tensor(parts[1][:, kt, :], t_bank[t % 2][:, :], parts[0][:, kt, :].bitcast(F32),
                                              ALU.subtract).then_inc(t_split, 1)
                    dve.wait_ge(bv_loaded, 16)
                    dve.wait_ge(vectors_ready, 1)

                    def round_of(r):
                        for kt in range(KT):
                            dve.wait_ge(t_hi, T_HEAD + KT * r + kt)
                            dve.tensor_tensor(ctxT[1][:, kt, :], t_bank[(T_HEAD + kt) % 2][:, 0:CB * M],
                                              ctxT[0][:, kt, :].bitcast(F32), ALU.subtract).then_inc(t_split, 1)
                        for g in range(G):
                            dve.wait_ge(m_hi, M_ROUND * r + g + 1)
                            dve.scalar_tensor_tensor(out=kT[:, g, 1, :], in0=m_bank[g % 2][:, 0:CB * M],
                                                     scalar=bk_col[:, g:g + 1], in1=kT[:, g, 0, :].bitcast(F32),
                                                     op0=ALU.add, op1=ALU.subtract).then_inc(m_split, 1)
                        for j in range(CB):
                            dve.wait_ge(m_full, M_ROUND * r + G + j + 1)
                            dve.tensor_tensor(v_sum[j % 2][:, :], m_bank[(G + j) % 2][0:M, :], bv_rows[:, :], ALU.add)\
                               .then_inc(v_summed, 1)
                            dve.wait_ge(m_hi, M_ROUND * r + G + j + 1)
                            dve.tensor_tensor(v_split[j % 2][:, 1, :], v_sum[j % 2][:, :],
                                              v_split[j % 2][:, 0, :].bitcast(F32), ALU.subtract).then_inc(m_split, 1)

                    with dve.Fori(0, ROUNDS) as r:
                        round_of(r)

        def attention(st, wqT, woT):
            x_in = sb(st, "x_in", [P, NT, D])
            stats = sb(st, "stats", [P, NT, 6])
            moments = sb(st, "moments", [P, 3, NT])
            mean = sb(st, "mean", [P, NT])
            var_eps = sb(st, "var_eps", [P, NT])
            rstd = sb(st, "rstd", [P, NT])
            xT = [sb(st, f"xT{i}", [P, KT, N], F32R) for i in range(2)]
            qT = [[sb(st, f"qT{s}_{i}", [P, N], F32R) for i in range(2)] for s in range(2)]
            k_diag = sb(st, "k_diag", [P, G, 2, GC], F32R)
            v_diag = sb(st, "v_diag", [P, G, 2, NC, P], F32R)
            peak = [sb(st, f"peak{i}", [P, UR]) for i in range(2)]
            exp_bias = [sb(st, f"exp_bias{i}", [P, UR]) for i in range(2)]
            exp_sum = [sb(st, f"exp_sum{i}", [P, UR]) for i in range(2)]
            exp_inv = [sb(st, f"exp_inv{i}", [P, UR]) for i in range(2)]
            exps = [sb(st, f"exps{i}", [P, HALF, GC]) for i in range(2)]
            probs = [sb(st, f"probs{g}", [P, NT, NC * P]) for g in range(G)]
            probsT = [sb(st, f"probsT{i}", [P, NC, N], F32R) for i in range(2)]
            oT = [sb(st, f"oT{i}", [P, G, N], F32R) for i in range(2)]
            residual = [sb(st, f"residual{t}", [P, D]) for t in range(NT)]
            bo_rows = sb(st, "bo_rows", [P, D])

            x_loaded = sem(st, "x_loaded")
            stats_ready = sem(st, "stats_ready")
            sums_ready = sem(st, "sums_ready")
            mean_ready = sem(st, "mean_ready")
            var_ready = sem(st, "var_ready")
            rstd_ready = sem(st, "rstd_ready")
            normed = sem(st, "normed")
            t_full = sem(st, "t_full_a")
            t_hi = sem(st, "t_hi_a")
            t_split = sem(st, "t_split_a")
            m_full = sem(st, "m_full_a")
            m_hi = sem(st, "m_hi_a")
            m_split = sem(st, "m_split_a")
            scores_full = sem(st, "scores_full")
            peak_ready = sem(st, "peak_ready")
            bias_ready = sem(st, "bias_ready")
            exps_ready = sem(st, "exps_ready")
            inv_ready = sem(st, "inv_ready")
            probs_ready = sem(st, "probs_ready")
            keys_loaded = [sem(st, f"keys_loaded{g}") for g in range(G)]
            values_loaded = [sem(st, f"values_loaded{g}") for g in range(G)]
            cleared = sem(st, "cleared")
            bo_loaded = sem(st, "bo_loaded")
            bo_gated = sem(st, "bo_gated")
            residual_loaded = [sem(st, f"residual_loaded{t}") for t in range(NT)]
            residual_ready = sem(st, "residual_ready")
            y_stored = [sem(st, f"y_stored{t}") for t in range(NT)]

            pieces = []
            for j in range(HG):
                r = j * M
                while r < (j + 1) * M:
                    n = min((j + 1) * M, (r // P + 1) * P) - r
                    pieces.append((j, r // P, r % P, r - j * M, n))
                    r += n

            T_TURN = G * NC + KT
            T_BEFORE = KT - 2 * NC
            M_TURN = 2 * G + NT
            M_BEFORE = 1 - 2 - NT
            H_TURN = 2 * G
            H_BEFORE = 1 - 2

            def counts(b, first):
                if first:
                    return Count(KT, KT % 2), Count(1, 1), Count(1, 1)
                return (Count(b * T_TURN + T_BEFORE, T_BEFORE % 2), Count(b * M_TURN + M_BEFORE, M_BEFORE % 2),
                        Count(b * H_TURN + H_BEFORE, H_BEFORE % 2))

            def scores_view(half):
                return pair_bank[half][:, :, 0:GC].rearrange("p n (h m) -> p n h m", m=M)

            block = st.enter_context(nc.Block())

            @block.sync
            def _(sp):
                def load_x(b):
                    sp.dma_start(x_in[:, :, :], x_tiles[b]).then_inc(x_loaded, 16)

                def load_keys(b, g):
                    for j in range(HG):
                        rows = slice(j * DH, (j + 1) * DH)
                        sp.dma_start(k_diag[rows, g, :, j * M:(j + 1) * M].bitcast(F32), k_parts[b, g, rows])\
                          .then_inc(keys_loaded[g], 16)

                def load_values(b, g):
                    for j, c, p0, m0, n in pieces:
                        cols = slice(g * P + j * DH, g * P + (j + 1) * DH)
                        sp.dma_start(v_diag[p0:p0 + n, g, :, c, j * DH:(j + 1) * DH].bitcast(F32),
                                     v_parts[b, m0:m0 + n, :, cols]).then_inc(values_loaded[g], 16)

                def load_residual(b):
                    for t in range(NT):
                        sp.dma_start(residual[t][:, :], x_tiles[b, :, t]).then_inc(residual_loaded[t], 16)

                def store_y(b, m, m_first):
                    for t in range(NT):
                        sp.wait_ge(m_split, m_first + t)
                        sp.dma_start(x1_tiles[b, :, t], residual[t][:, :]).then_inc(y_stored[t], 16)

                def turn(b, first, last):
                    t, m, _ = counts(b, first)
                    if not last:
                        if not first:
                            sp.wait_ge(t_full, t.done)
                        load_x(b + 1)
                    for g in range(G):
                        if not last:
                            sp.wait_ge(scores_full, 2 * G * b + 2 * g + 2)
                            load_keys(b + 1, g)
                        if g == 2 and not first:
                            outs = [m.next()[0]]
                            m.next()
                            outs += [m.next()[0] for _ in range(NT - 1)]
                            for tile in range(NT):
                                sp.wait_ge(m_split, outs[tile])
                                sp.dma_start(x1_tiles[b - 1, :, tile], residual[tile][:, :])\
                                  .then_inc(y_stored[tile], 16)
                        elif not (last and g == 3):
                            m.next()
                        if g == 2:
                            for tile in range(NT):
                                if not first:
                                    sp.wait_ge(y_stored[tile], 16 * b)
                                sp.dma_start(residual[tile][:, :], x_tiles[b, :, tile])\
                                  .then_inc(residual_loaded[tile], 16)
                        if not (first and g < 2):
                            value_product = m.next()[0]
                            done = b - 1 if g < 2 else b
                            if not (last and g >= 2):
                                sp.wait_ge(m_full, value_product)
                                load_values(done + 1, (g + 2) % G)

                for t_ in (bo_rows,):
                    sp.dma_start(t_[:, :], bo.rearrange("(a d) -> a d", a=1).to_broadcast([P, D])).then_inc(bo_loaded, 16)
                load_x(0)
                sp.wait_ge(cleared, 1)
                for g in range(G):
                    load_keys(0, g)
                for g in range(G):
                    load_values(0, g)
                sp.wait_ge(t_full, KT)
                turn(0, True, False)
                with sp.Fori(1, B - 1) as b:
                    turn(b, False, False)
                turn(B - 1, False, True)
                t, m, _ = counts(B, False)
                for tile in range(NT):
                    sp.wait_ge(m_split, B * M_TURN + M_BEFORE - 1 + 2 + tile + 1)
                    sp.dma_start(x1_tiles[B - 1, :, tile], residual[tile][:, :]).then_inc(y_stored[tile], 16)
                for tile in range(NT):
                    sp.wait_ge(y_stored[tile], 16 * B)

            @block.gpsimd
            def _(pool):
                pool.wait_ge(bo_loaded, 16)
                pool.tensor_scalar(bo_rows[:, :], bo_rows[:, :], tanh_g[:, 0:1], 0.0, ALU.mult, ALU.add)\
                    .then_inc(bo_gated, 1)

                def rstd_of(n):
                    pool.wait_ge(var_ready, n)
                    pool.tensor_tensor(rstd[:, :], var_eps[:, :], minus_half[:, :], ALU.pow).then_inc(rstd_ready, 1)

                def turn(b, first, last):
                    for g in range(G):
                        for half in range(2):
                            pool.wait_ge(inv_ready, 2 * G * b + 2 * g + half + 1)
                            pool.tensor_tensor(
                                probs[g][:, HALF * half:HALF * (half + 1), 0:GC].rearrange("p n (h m) -> p n h m", m=M),
                                exps[half][:, :, :].rearrange("p n (h m) -> p n h m", m=M),
                                exp_inv[half][:, :].rearrange("p (n h o) -> p n h o", h=HG, o=1)
                                .to_broadcast([P, HALF, HG, M]),
                                ALU.mult).then_inc(probs_ready, 1)
                        if g == 1 and not last:
                            rstd_of(b + 2)
                        if g == 0 and not first:
                            add_bias(b - 1)

                def add_bias(b):
                    for tile in range(NT):
                        pool.wait_ge(residual_loaded[tile], 16 * (b + 1))
                        if tile == 0:
                            pool.wait_ge(bo_gated, 1)
                        pool.tensor_tensor(residual[tile][:, :], residual[tile][:, :], bo_rows[:, :], ALU.add)\
                            .then_inc(residual_ready, 1)

                rstd_of(1)
                turn(0, True, False)
                with pool.Fori(1, B - 1) as b:
                    turn(b, False, False)
                turn(B - 1, False, True)
                add_bias(B - 1)

            @block.tensor
            def _(pe):
                def transpose_x(kt, n, bank, b_next):
                    if kt == 0:
                        pe.wait_ge(normed, NT * (b_next + 1))
                    if not (isinstance(n, int) and n <= 2):
                        pe.wait_ge(t_split, n - 2)
                    for tile in range(NT):
                        tr = pe.transpose(t_bank[bank][:, tile * P:(tile + 1) * P],
                                          x_in[:, tile, kt * P:(kt + 1) * P], ident[:, :])
                    tr.then_inc(t_full, 1)

                def transpose_probs(g, c, n, bank, units):
                    if c == 0:
                        pe.wait_ge(probs_ready, units)
                    pe.wait_ge(t_split, n - 2)
                    for tile in range(NT):
                        tr = pe.transpose(t_bank[bank][:, tile * P:(tile + 1) * P],
                                          probs[g][:, tile, c * P:(c + 1) * P], ident[:, :])
                    tr.then_inc(t_full, 1)

                def queries(g, n, bank, kts, x_split=None):
                    if kts[0] == 0:
                        if x_split is not None:
                            pe.wait_ge(t_split, x_split)
                        if not (isinstance(n, int) and n <= 2):
                            pe.wait_ge(m_split, n - 2)
                    for kt in kts:
                        mm = matmul3(pe, m_bank[bank][:, :], lambda p: wqT[p][:, kt, g * P:(g + 1) * P],
                                     lambda p: xT[p][:, kt, :], kt == 0, kt == KT - 1)
                    if kts[-1] == KT - 1:
                        mm.then_inc(m_full, 1)

                def scores(b, g, half, q_split, first):
                    if half == 0:
                        pe.wait_ge(m_split, q_split)
                        pe.wait_ge(keys_loaded[g], 16 * HG * (b + 1))
                    if not (first and g == 0):
                        pe.wait_ge(exps_ready, 2 * G * b + 2 * g + half - 1)
                    for n in range(HALF):
                        tile = HALF * half + n
                        mm = matmul3(pe, pair_bank[half][:, n, 0:GC],
                                     lambda p: qT[g % 2][p][:, tile * P:(tile + 1) * P],
                                     lambda p: k_diag[:, g, p, :], True, True)
                    mm.then_inc(scores_full, 1)

                def value_product(b, g, n, bank, t_done):
                    pe.wait_ge(t_split, t_done)
                    pe.wait_ge(values_loaded[g], 16 * len(pieces) * (b + 1))
                    pe.wait_ge(m_split, n - 2)
                    for c in range(NC):
                        mm = matmul3(pe, m_bank[bank][:, :], lambda p: v_diag[:, g, p, c, :],
                                     lambda p: probsT[p][:, c, :], c == 0, c == NC - 1)
                    mm.then_inc(m_full, 1)

                def block_output(tile, n, bank, o_split=None):
                    if o_split is not None:
                        pe.wait_ge(m_split, o_split)
                    pe.wait_ge(m_split, n - 2)
                    for g in range(G):
                        mm = matmul3(pe, m_bank[bank][:, :], lambda p: oT[p][:, g, tile * P:(tile + 1) * P],
                                     lambda p: woT[p][:, g, :], g == 0, g == G - 1)
                    mm.then_inc(m_full, 1)

                def turn(b, first, last):
                    t, m, _ = counts(b, first)
                    for g in range(G):
                        back, back_g = (b - 1, g + 2) if g < 2 else (b, g - 2)
                        units = 2 * G * b + 2 * g - 2
                        finish = not (first and g < 2)
                        project = not (last and g == 3)
                        q_split = m.done + m.uses - (0 if first and g <= 2 else 1)
                        if g == 3 and not last:
                            for kt in range(2):
                                transpose_x(kt, *t.next(), b + 1)
                        if g < 3 and finish:
                            for c in range(2):
                                transpose_probs(back_g, c, *t.next(), units)
                        scores(b, g, 0, q_split, first)
                        if g == 3 and not last:
                            transpose_x(2, *t.next(), b + 1)
                        scores(b, g, 1, q_split, first)
                        x_split = None
                        if g == 3:
                            if not last:
                                n, bank = t.next()
                                transpose_x(3, n, bank, b + 1)
                                x_split = n
                            for c in range(2):
                                transpose_probs(back_g, c, *t.next(), units)
                        if g == 2 and not first:
                            n, bank = m.next()
                            block_output(0, n, bank, n - 1)
                        if project:
                            n, bank = m.next()
                            queries((g + 1) % G, n, bank, (0, 1), x_split)
                        if finish:
                            t_done, t_slot = t.next()
                            transpose_probs(back_g, 2, t_done, t_slot, units)
                        if project:
                            queries((g + 1) % G, n, bank, (2, 3))
                        if g == 2 and not first:
                            for tile in range(1, NT):
                                block_output(tile, *m.next())
                        if finish:
                            value_product(back, back_g, *m.next(), t_done)

                for kt in range(KT):
                    transpose_x(kt, kt + 1, kt % 2, 0)
                queries(0, 1, 0, (0, 1, 2, 3), KT)
                turn(0, True, False)
                with pe.Fori(1, B - 1) as b:
                    turn(b, False, False)
                turn(B - 1, False, True)
                t, m = Count(B * T_TURN + T_BEFORE - KT, (T_BEFORE - KT) % 2), Count(B * M_TURN + M_BEFORE - 1, (M_BEFORE - 1) % 2)
                for g in (2, 3):
                    for c in range(NC):
                        t_done, t_slot = t.next()
                        transpose_probs(g, c, t_done, t_slot, 2 * G * B)
                    value_product(B - 1, g, *m.next(), t_done)
                for tile in range(NT):
                    n, bank = m.next()
                    block_output(tile, n, bank, n - 1 if tile == 0 else None)

            @block.scalar
            def _(act):
                def bank_hi(dst, n, bank):
                    act.wait_ge(t_full, n)
                    act.activation(dst, t_bank[bank][:, :], ACT.Copy).then_inc(t_hi, 1)

                def exponentials(unit, half):
                    act.wait_ge(bias_ready, unit)
                    if not (isinstance(unit, int) and unit <= 2):
                        act.wait_ge(probs_ready, unit - 2)
                    for i in range(UR):
                        n, h = i // HG, i % HG
                        e = act.activation(exps[half][:, n, h * M:(h + 1) * M], pair_bank[half][:, n, h * M:(h + 1) * M],
                                           ACT.Exp, bias=exp_bias[half][:, i:i + 1], scale=SCALE,
                                           accum_out=exp_sum[half][:, i:i + 1])
                    e.then_inc(exps_ready, 1)

                def turn(b, first, last):
                    t, m, _ = counts(b, first)
                    for g in range(G):
                        back_g = (g + 2) % G
                        finish = not (first and g < 2)
                        unit = 2 * G * b + 2 * g
                        if g == 3 and not last:
                            for kt in range(KT):
                                bank_hi(xT[0][:, kt, :], *t.next())
                        if g < 3 and finish:
                            for c in range(2):
                                bank_hi(probsT[0][:, c, :], *t.next())
                        exponentials(unit + 1, 0)
                        if g == 3:
                            for c in range(2):
                                bank_hi(probsT[0][:, c, :], *t.next())
                        if g == 2 and not first:
                            m.next()
                        if finish:
                            bank_hi(probsT[0][:, 2, :], *t.next())
                        if not (last and g == 3):
                            n, bank = m.next()
                            act.wait_ge(m_full, n)
                            q = (g + 1) % G
                            act.activation(qT[q % 2][0][:, :], m_bank[bank][:, :], ACT.Identity,
                                           bias=bq_col[:, q:q + 1]).then_inc(m_hi, 1)
                        exponentials(unit + 2, 1)
                        if g == 2 and not first:
                            for _ in range(1, NT):
                                m.next()
                        if finish:
                            n, bank = m.next()
                            act.wait_ge(m_full, n)
                            act.activation(oT[0][:, back_g, :], m_bank[bank][:, :], ACT.Copy).then_inc(m_hi, 1)

                for kt in range(KT):
                    bank_hi(xT[0][:, kt, :], kt + 1, kt % 2)
                act.wait_ge(m_full, 1)
                act.activation(qT[0][0][:, :], m_bank[0][:, :], ACT.Identity, bias=bq_col[:, 0:1]).then_inc(m_hi, 1)
                turn(0, True, False)
                with act.Fori(1, B - 1) as b:
                    turn(b, False, False)
                turn(B - 1, False, True)
                t, m = Count(B * T_TURN + T_BEFORE - KT, (T_BEFORE - KT) % 2), Count(B * M_TURN + M_BEFORE - 1, (M_BEFORE - 1) % 2)
                for g in (2, 3):
                    for c in range(NC):
                        bank_hi(probsT[0][:, c, :], *t.next())
                    n, bank = m.next()
                    act.wait_ge(m_full, n)
                    act.activation(oT[0][:, g, :], m_bank[bank][:, :], ACT.Copy).then_inc(m_hi, 1)

            @block.vector
            def _(dve):
                def bank_lo(dst, hi, n, bank):
                    dve.wait_ge(t_hi, n)
                    dve.tensor_tensor(dst, t_bank[bank][:, :], hi.bitcast(F32), ALU.subtract).then_inc(t_split, 1)

                def probs_lo(c, n, bank):
                    bank_lo(probsT[1][:, c, :], probsT[0][:, c, :], n, bank)

                def peaks(unit, half):
                    dve.wait_ge(scores_full, unit)
                    dve.tensor_reduce(peak[half][:, :].rearrange("p (n h) -> p n h", h=HG), scores_view(half),
                                      AX_X, ALU.max).then_inc(peak_ready, 1)
                    dve.wait_ge(peak_ready, unit)
                    dve.tensor_scalar(exp_bias[half][:, :], peak[half][:, :], -SCALE, None, ALU.mult)\
                       .then_inc(bias_ready, 1)

                def inverse(unit, half):
                    dve.wait_ge(exps_ready, unit)
                    dve.reciprocal(exp_inv[half][:, :], exp_sum[half][:, :]).then_inc(inv_ready, 1)

                def statistics(n):
                    dve.wait_ge(x_loaded, 16 * n)
                    for tile in range(NT):
                        dve.bn_stats(stats[:, tile, :], x_in[:, tile, :]).then_inc(stats_ready, 1)
                    dve.wait_ge(stats_ready, NT * n)
                    dve.tensor_tensor(moments[:, 0, :], stats[:, :, 1], stats[:, :, 4], ALU.add)
                    dve.tensor_tensor(moments[:, 1, :], stats[:, :, 1], stats[:, :, 4], ALU.subtract)
                    dve.tensor_tensor(moments[:, 2, :], stats[:, :, 2], stats[:, :, 5], ALU.add)\
                       .then_inc(sums_ready, 1)
                    dve.wait_ge(sums_ready, n)
                    dve.tensor_scalar(mean[:, :], moments[:, 0, :], 0.5, None, ALU.mult)
                    dve.scalar_tensor_tensor(out=moments[:, 1, :], in0=moments[:, 1, :], scalar=0.25,
                                             in1=moments[:, 1, :], op0=ALU.mult, op1=ALU.mult)
                    dve.tensor_scalar(moments[:, 2, :], moments[:, 2, :], 1.0 / D, EPS, ALU.mult, ALU.add)\
                       .then_inc(mean_ready, 1)
                    dve.wait_ge(mean_ready, n)
                    dve.tensor_tensor(var_eps[:, :], moments[:, 1, :], moments[:, 2, :], ALU.add).then_inc(var_ready, 1)

                def normalise(n):
                    dve.wait_ge(rstd_ready, n)
                    for tile in range(NT):
                        dve.tensor_scalar(x_in[:, tile, :], x_in[:, tile, :], mean[:, tile:tile + 1],
                                          rstd[:, tile:tile + 1], ALU.subtract, ALU.mult).then_inc(normed, 1)

                def queries_lo(q, n, bank, h):
                    dve.wait_ge(m_hi, h)
                    dve.scalar_tensor_tensor(out=qT[q % 2][1][:, :], in0=m_bank[bank][:, :], scalar=bq_col[:, q:q + 1],
                                             in1=qT[q % 2][0][:, :].bitcast(F32), op0=ALU.add, op1=ALU.subtract)\
                       .then_inc(m_split, 1)

                def heads_lo(g, n, bank, h):
                    dve.wait_ge(m_hi, h)
                    dve.tensor_tensor(oT[1][:, g, :], m_bank[bank][:, :], oT[0][:, g, :].bitcast(F32), ALU.subtract)\
                       .then_inc(m_split, 1)

                def gate_output(b, tile, n, bank):
                    dve.wait_ge(m_full, n)
                    dve.wait_ge(residual_ready, NT * b + tile + 1)
                    dve.scalar_tensor_tensor(out=residual[tile][:, :], in0=m_bank[bank][:, :], scalar=tanh_g[:, 0:1],
                                             in1=residual[tile][:, :], op0=ALU.mult, op1=ALU.add).then_inc(m_split, 1)

                def turn(b, first, last):
                    t, m, h = counts(b, first)
                    for g in range(G):
                        back_g = (g + 2) % G
                        finish = not (first and g < 2)
                        unit = 2 * G * b + 2 * g
                        if g == 3:
                            if not last:
                                for kt in range(2):
                                    bank_lo(xT[1][:, kt, :], xT[0][:, kt, :], *t.next())
                            peaks(unit + 1, 0)
                            if not last:
                                bank_lo(xT[1][:, 2, :], xT[0][:, 2, :], *t.next())
                            peaks(unit + 2, 1)
                            if not last:
                                bank_lo(xT[1][:, 3, :], xT[0][:, 3, :], *t.next())
                            inverse(unit + 1, 0)
                            for c in range(2):
                                probs_lo(c, *t.next())
                        else:
                            if finish:
                                for c in range(2):
                                    probs_lo(c, *t.next())
                            peaks(unit + 1, 0)
                            peaks(unit + 2, 1)
                        if g == 2 and not first:
                            gate_output(b - 1, 0, *m.next())
                        if g < 3:
                            inverse(unit + 1, 0)
                        if finish:
                            probs_lo(2, *t.next())
                        if not (last and g == 3):
                            queries_lo((g + 1) % G, *m.next(), h.next()[0])
                        inverse(unit + 2, 1)
                        if g == 2 and not first:
                            for tile in range(1, NT):
                                gate_output(b - 1, tile, *m.next())
                        if finish:
                            heads_lo(back_g, *m.next(), h.next()[0])
                        if g == 1 and not last:
                            statistics(b + 2)
                        if g == 2 and not last:
                            normalise(b + 2)

                dve.memset(k_diag[:, :, :, :].bitcast(F32), 0.0)
                for g in range(G):
                    dve.memset(probs[g][:, :, GC:NC * P], 0.0)
                dve.memset(v_diag[:, :, :, :, :].bitcast(F32), 0.0).then_inc(cleared, 1)
                statistics(1)
                normalise(1)
                for kt in range(KT):
                    bank_lo(xT[1][:, kt, :], xT[0][:, kt, :], kt + 1, kt % 2)
                queries_lo(0, 1, 0, 1)
                turn(0, True, False)
                with dve.Fori(1, B - 1) as b:
                    turn(b, False, False)
                turn(B - 1, False, True)
                t, m = Count(B * T_TURN + T_BEFORE - KT, (T_BEFORE - KT) % 2), Count(B * M_TURN + M_BEFORE - 1, (M_BEFORE - 1) % 2)
                h = Count(B * H_TURN + H_BEFORE - 1, (H_BEFORE - 1) % 2)
                for g in (2, 3):
                    for c in range(NC):
                        probs_lo(c, *t.next())
                    heads_lo(g, *m.next(), h.next()[0])
                for tile in range(NT):
                    gate_output(B - 1, tile, *m.next())

        def ffn_setup(st, w1_split, w2_split, turns_phase, sine_gain, b2_rows):
            CHUNK = KT * D
            raw = [sb(st, f"w_chunk{i}", [P, CHUNK]) for i in range(2)]
            work = [sb(st, f"phase_work{i}", [P, FT]) for i in range(4)]
            raw_loaded = [sem(st, f"raw_loaded{i}") for i in range(2)]
            hi_ready = sem(st, "chunk_hi")
            split = sem(st, "chunk_split")
            b2_loaded = sem(st, "b2_loaded")
            b2_gated = sem(st, "b2_gated")
            step = sem(st, "phase_step")
            sines_ready = sem(st, "sines_ready")

            w1_rows = w1.rearrange("(k p) f -> k p f", p=P)
            w2_rows = w2.rearrange("(c f p) d -> c p f d", p=P, f=KT)
            chunks = [(w1_rows[k], w1_split[0][:, k, :], w1_split[1][:, k, :], None) for k in range(KT)]
            chunks += [(w2_rows[c], *(w2_split[i][:, KT * c:KT * (c + 1), :].rearrange("p f d -> p (f d)")
                                      for i in range(2)), D) for c in range(FT // KT)]

            block = st.enter_context(nc.Block())

            @block.sync
            def _(sp):
                sp.dma_start(b2_rows[:, :], b2.rearrange("(a d) -> a d", a=1).to_broadcast([P, D])).then_inc(b2_loaded, 16)
                for n, (source, _, _, rows) in enumerate(chunks):
                    if n >= 2:
                        sp.wait_ge(split, n - 1)
                    to = raw[n % 2][:, :]
                    if rows:
                        to = to.rearrange("p (f d) -> p f d", d=rows)
                    sp.dma_start(to, source).then_inc(raw_loaded[n % 2], 16)

            @block.scalar
            def _(act):
                act.wait_ge(step, 9)
                act.activation(work[2][:, :], turns_phase[:, :], ACT.Sin, scale=TWO_PI_BELOW)
                act.activation(work[3][:, :], work[1][:, :], ACT.Sin, scale=TWO_PI_BELOW).then_inc(sines_ready, 1)
                for n, (_, hi, _, _) in enumerate(chunks):
                    act.wait_ge(raw_loaded[n % 2], 16 * (n // 2 + 1))
                    act.activation(hi, raw[n % 2][:, :], ACT.Copy).then_inc(hi_ready, 1)

            @block.gpsimd
            def _(pool):
                pool.wait_ge(b2_loaded, 16)
                pool.tensor_scalar(b2_rows[:, :], b2_rows[:, :], tanh_g[:, 1:2], 0.0, ALU.mult, ALU.add)\
                    .then_inc(b2_gated, 1)

            @block.vector
            def _(dve):
                steps = [0]

                def stepped(instruction):
                    steps[0] += 1
                    instruction.then_inc(step, 1)
                    dve.wait_ge(step, steps[0])

                stepped(dve.tensor_scalar(work[0][:, :], phase_col, 1.0 / TWO_PI, ROUND_MAGIC, ALU.mult, ALU.add))
                stepped(dve.tensor_scalar(work[0][:, :], work[0][:, :], ROUND_MAGIC, None, ALU.subtract))
                stepped(dve.scalar_tensor_tensor(out=work[1][:, :], in0=work[0][:, :], scalar=-TWO_PI_PARTS[0],
                                                 in1=phase_col, op0=ALU.mult, op1=ALU.add))
                stepped(dve.scalar_tensor_tensor(out=work[1][:, :], in0=work[0][:, :], scalar=-TWO_PI_PARTS[1],
                                                 in1=work[1][:, :], op0=ALU.mult, op1=ALU.add))
                stepped(dve.scalar_tensor_tensor(out=work[1][:, :], in0=work[0][:, :], scalar=-TWO_PI_PARTS[2],
                                                 in1=work[1][:, :], op0=ALU.mult, op1=ALU.add))
                stepped(dve.tensor_scalar(work[1][:, :], work[1][:, :], 1.0 / TWO_PI, 0.5, ALU.mult, ALU.min))
                stepped(dve.tensor_scalar(turns_phase[:, :], work[1][:, :], -0.5, None, ALU.max))
                stepped(dve.tensor_scalar(work[0][:, :], turns_phase[:, :], 0.25, -1.0, ALU.is_gt, ALU.mult))
                stepped(dve.scalar_tensor_tensor(out=work[1][:, :], in0=turns_phase[:, :], scalar=0.25,
                                                 in1=work[0][:, :], op0=ALU.add, op1=ALU.add))
                dve.wait_ge(sines_ready, 1)
                stepped(dve.scalar_tensor_tensor(out=turns_phase[:, :], in0=b1_col, scalar=0.1 / TWO_PI,
                                                 in1=turns_phase[:, :], op0=ALU.mult, op1=ALU.add))
                stepped(dve.tensor_tensor(work[3][:, :], work[3][:, :], real_col, ALU.mult))
                stepped(dve.tensor_tensor(work[2][:, :], work[2][:, :], imag_col, ALU.mult))
                stepped(dve.tensor_tensor(work[3][:, :], work[3][:, :], work[2][:, :], ALU.add))
                stepped(dve.scalar_tensor_tensor(out=sine_gain[:, :], in0=work[3][:, :], scalar=0.1,
                                                 in1=imag_col, op0=ALU.mult, op1=ALU.mult))
                for n, (_, hi, lo, _) in enumerate(chunks):
                    dve.wait_ge(hi_ready, n + 1)
                    dve.tensor_tensor(lo, raw[n % 2][:, :], hi.bitcast(F32), ALU.subtract).then_inc(split, 1)

        def ffn(st, w1_split, w2_split, turns_phase, sine_gain, b2_rows):
            AHEAD = 2
            LN_AT, NORM_AT, XT_AT = 3, 6, 9
            x_in = sb(st, "x1_in", [P, NT, D])
            stats = sb(st, "stats1", [P, NT, 6])
            moments = sb(st, "moments1", [P, 3, NT])
            mean = sb(st, "mean1", [P, NT])
            var_eps = sb(st, "var_eps1", [P, NT])
            rstd = sb(st, "rstd1", [P, NT])
            xT = [[sb(st, f"x1T{s}_{i}", [P, KT, N], F32R) for i in range(2)] for s in range(2)]
            hidden = [sb(st, f"hidden{i}", [P, N]) for i in range(2)]
            turns = sb(st, "turns", [P, N])
            sine = sb(st, "sine", [P, N])
            relu = [[sb(st, f"relu{s}_{i}", [P, N], F32R) for i in range(2)] for s in range(2)]
            residual = [sb(st, f"residual1_{t}", [P, D]) for t in range(NT)]

            x_loaded = sem(st, "x1_loaded")
            stats_ready = sem(st, "stats_ready1")
            sums_ready = sem(st, "sums_ready1")
            mean_ready = sem(st, "mean_ready1")
            var_ready = sem(st, "var_ready1")
            rstd_ready = sem(st, "rstd_ready1")
            normed = sem(st, "normed1")
            t_full = sem(st, "t_full_f")
            t_hi = sem(st, "t_hi_f")
            t_split = sem(st, "t_split_f")
            h_full = sem(st, "h_full")
            h_ready = sem(st, "h_ready")
            whole_ready = sem(st, "whole_ready")
            part_ready = sem(st, "part_ready")
            sine_ready = sem(st, "sine_ready")
            mixed = sem(st, "mixed")
            relu_hi = sem(st, "relu_hi")
            relu_split = sem(st, "relu_split")
            relu_used = sem(st, "relu_used")
            y_full = sem(st, "y_full")
            y_ready = sem(st, "y_ready")
            residual_loaded = [sem(st, f"residual_loaded1_{t}") for t in range(NT)]
            residual_ready = sem(st, "residual_ready1")
            y_stored = [sem(st, f"y_stored1_{t}") for t in range(NT)]

            block = st.enter_context(nc.Block())

            def over_batches(eng, batch):
                with eng.Fori(0, B - 2, 2) as b:
                    batch(b, 0, False)
                    batch(b + 1, 1, False)
                batch(B - 2, 0, False)
                batch(B - 1, 1, True)

            @block.sync
            def _(sp):
                def load_x(b):
                    sp.dma_start(x_in[:, :, :], x1_tiles[b]).then_inc(x_loaded, 16)

                def load_residual(b, tile):
                    sp.dma_start(residual[tile][:, :], x1_tiles[b, :, tile]).then_inc(residual_loaded[tile], 16)

                def store_y(b, tile):
                    sp.wait_ge(y_ready, NT * (b + 1) + tile + 1)
                    sp.dma_start(out_tiles[b, :, tile], residual[tile][:, :]).then_inc(y_stored[tile], 16)

                load_x(0)
                for tile in range(NT):
                    load_residual(0, tile)
                sp.wait_ge(t_full, KT)
                load_x(1)

                def batch(b):
                    sp.wait_ge(t_full, KT * (b + 2))
                    load_x(b + 2)
                    for tile in range(NT):
                        store_y(b, tile)
                    for tile in range(NT):
                        sp.wait_ge(y_stored[tile], 16 * (b + 1))
                        load_residual(b + 1, tile)

                with sp.Fori(0, B - 2) as b:
                    batch(b)
                for tile in range(NT):
                    store_y(B - 2, tile)
                for tile in range(NT):
                    sp.wait_ge(y_stored[tile], 16 * (B - 1))
                    load_residual(B - 1, tile)
                for tile in range(NT):
                    store_y(B - 1, tile)
                for tile in range(NT):
                    sp.wait_ge(y_stored[tile], 16 * B)

            @block.gpsimd
            def _(pool):
                def rstd_of(n):
                    pool.wait_ge(var_ready, n)
                    pool.tensor_tensor(rstd[:, :], var_eps[:, :], minus_half[:, :], ALU.pow).then_inc(rstd_ready, 1)

                def batch(b, slot, last):
                    if not last:
                        rstd_of(b + 2)
                    for tile in range(NT):
                        pool.wait_ge(residual_loaded[tile], 16 * (b + 1))
                        pool.tensor_tensor(residual[tile][:, :], residual[tile][:, :], b2_rows[:, :], ALU.add)\
                            .then_inc(residual_ready, 1)

                rstd_of(1)
                over_batches(pool, batch)

            @block.tensor
            def _(pe):
                def transpose_x(b, slot):
                    pe.wait_ge(normed, NT * (b + 1))
                    for kt in range(KT):
                        if not (isinstance(b, int) and b == 0 and kt < 2):
                            pe.wait_ge(t_split, KT * b + kt - 1)
                        for tile in range(NT):
                            tr = pe.transpose(t_bank[kt % 2][:, tile * P:(tile + 1) * P],
                                              x_in[:, tile, kt * P:(kt + 1) * P], ident[:, :])
                        tr.then_inc(t_full, 1)

                def first_product(b, slot, f):
                    if f == 0:
                        pe.wait_ge(t_split, KT * (b + 1))
                    if not (isinstance(b, int) and b == 0 and f < 2):
                        pe.wait_ge(h_ready, FT * b + f - 1)
                    for kt in range(KT):
                        mm = matmul3(pe, m_bank[f % 2][:, :], lambda p: w1_split[p][:, kt, f * P:(f + 1) * P],
                                     lambda p: xT[slot][p][:, kt, :], kt == 0, kt == KT - 1)
                    mm.then_inc(h_full, 1)

                def second_product(b, f):
                    pe.wait_ge(relu_split, FT * b + f + 1)
                    for tile in range(NT):
                        if f == 0:
                            pe.wait_ge(y_ready, NT * b + tile + 1)
                        mm = matmul3(pe, pair_bank[tile // 2][:, tile % 2, :],
                                     lambda p: relu[f % 2][p][:, tile * P:(tile + 1) * P],
                                     lambda p: w2_split[p][:, f, :], f == 0, f == FT - 1)
                        if f == FT - 1:
                            mm.then_inc(y_full, 1)
                    if f < FT - 1:
                        mm.then_inc(relu_used, 1)

                def batch(b, slot, last):
                    for f in range(FT):
                        ahead = f + AHEAD
                        if ahead < FT:
                            first_product(b, slot, ahead)
                        elif not last:
                            first_product(b + 1, 1 - slot, ahead - FT)
                        second_product(b, f)
                        if f == XT_AT and not last:
                            transpose_x(b + 1, 1 - slot)

                transpose_x(0, 0)
                for f in range(AHEAD):
                    first_product(0, 0, f)
                over_batches(pe, batch)

            @block.scalar
            def _(act):
                def x_hi(b, slot):
                    for kt in range(KT):
                        act.wait_ge(t_full, KT * b + kt + 1)
                        act.activation(xT[slot][0][:, kt, :], t_bank[kt % 2][:, :], ACT.Copy).then_inc(t_hi, 1)

                def relu_of(b, f):
                    act.wait_ge(mixed, FT * b + f + 1)
                    act.activation(relu[f % 2][0][:, :], hidden[f % 2][:, :], ACT.Relu).then_inc(relu_hi, 1)

                def step(b, f):
                    act.wait_ge(h_full, FT * b + f + 1)
                    if f:
                        relu_of(b, f - 1)
                    act.activation(hidden[f % 2][:, :], m_bank[f % 2][:, :], ACT.Identity,
                                   bias=b1_col[:, f % FT:f % FT + 1])
                    act.activation(turns[:, :], m_bank[f % 2][:, :], ACT.Identity, scale=0.1 / TWO_PI,
                                   bias=turns_phase[:, f % FT:f % FT + 1]).then_inc(h_ready, 1)
                    act.wait_ge(part_ready, FT * b + f + 1)
                    act.activation(sine[:, :], turns[:, :], ACT.Sin, scale=TWO_PI_BELOW).then_inc(sine_ready, 1)

                def batch(b, slot, last):
                    for f in range(1, FT):
                        step(b, f)
                        if f == XT_AT + AHEAD and not last:
                            x_hi(b + 1, 1 - slot)
                    if last:
                        act.wait_ge(relu_used, (FT - 1) * b + FT - 2)
                        relu_of(b, FT - 1)
                    else:
                        step(b, FT)

                x_hi(0, 0)
                step(0, 0)
                over_batches(act, batch)

            @block.vector
            def _(dve):
                def statistics(n):
                    dve.wait_ge(x_loaded, 16 * n)
                    for tile in range(NT):
                        dve.bn_stats(stats[:, tile, :], x_in[:, tile, :]).then_inc(stats_ready, 1)
                    dve.wait_ge(stats_ready, NT * n)
                    dve.tensor_tensor(moments[:, 0, :], stats[:, :, 1], stats[:, :, 4], ALU.add)
                    dve.tensor_tensor(moments[:, 1, :], stats[:, :, 1], stats[:, :, 4], ALU.subtract)
                    dve.tensor_tensor(moments[:, 2, :], stats[:, :, 2], stats[:, :, 5], ALU.add)\
                       .then_inc(sums_ready, 1)
                    dve.wait_ge(sums_ready, n)
                    dve.tensor_scalar(mean[:, :], moments[:, 0, :], 0.5, None, ALU.mult)
                    dve.scalar_tensor_tensor(out=moments[:, 1, :], in0=moments[:, 1, :], scalar=0.25,
                                             in1=moments[:, 1, :], op0=ALU.mult, op1=ALU.mult)
                    dve.tensor_scalar(moments[:, 2, :], moments[:, 2, :], 1.0 / D, EPS, ALU.mult, ALU.add)\
                       .then_inc(mean_ready, 1)
                    dve.wait_ge(mean_ready, n)
                    dve.tensor_tensor(var_eps[:, :], moments[:, 1, :], moments[:, 2, :], ALU.add).then_inc(var_ready, 1)

                def normalise(n):
                    dve.wait_ge(rstd_ready, n)
                    for tile in range(NT):
                        dve.tensor_scalar(x_in[:, tile, :], x_in[:, tile, :], mean[:, tile:tile + 1],
                                          rstd[:, tile:tile + 1], ALU.subtract, ALU.mult).then_inc(normed, 1)

                def x_lo(b, slot):
                    for kt in range(KT):
                        dve.wait_ge(t_hi, KT * b + kt + 1)
                        dve.tensor_tensor(xT[slot][1][:, kt, :], t_bank[kt % 2][:, :],
                                          xT[slot][0][:, kt, :].bitcast(F32), ALU.subtract).then_inc(t_split, 1)

                def relu_lo(b, f):
                    dve.wait_ge(relu_hi, FT * b + f + 1)
                    dve.scalar_tensor_tensor(out=relu[f % 2][1][:, :], in0=hidden[f % 2][:, :], scalar=0.0,
                                             in1=relu[f % 2][0][:, :].bitcast(F32), op0=ALU.max, op1=ALU.subtract)\
                       .then_inc(relu_split, 1)

                def step(b, f):
                    if f:
                        relu_lo(b, f - 1)
                    n = FT * b + f + 1
                    dve.wait_ge(h_ready, n)
                    dve.tensor_scalar(sine[:, :], turns[:, :], ROUND_MAGIC, ROUND_MAGIC, ALU.add, ALU.subtract)\
                       .then_inc(whole_ready, 1)
                    dve.wait_ge(whole_ready, n)
                    dve.tensor_tensor(turns[:, :], turns[:, :], sine[:, :], ALU.subtract).then_inc(part_ready, 1)
                    dve.wait_ge(sine_ready, n)
                    dve.scalar_tensor_tensor(out=hidden[f % 2][:, :], in0=sine[:, :],
                                             scalar=sine_gain[:, f % FT:f % FT + 1], in1=hidden[f % 2][:, :],
                                             op0=ALU.mult, op1=ALU.add).then_inc(mixed, 1)

                def outputs(b):
                    for tile in range(NT):
                        dve.wait_ge(y_full, NT * b + tile + 1)
                        dve.wait_ge(residual_ready, NT * b + tile + 1)
                        dve.scalar_tensor_tensor(out=residual[tile][:, :], in0=pair_bank[tile // 2][:, tile % 2, :],
                                                 scalar=tanh_g[:, 1:2], in1=residual[tile][:, :],
                                                 op0=ALU.mult, op1=ALU.add).then_inc(y_ready, 1)

                def batch(b, slot, last):
                    for f in range(1, FT):
                        step(b, f)
                        if not last:
                            if f == LN_AT:
                                statistics(b + 2)
                            if f == NORM_AT:
                                normalise(b + 2)
                            if f == XT_AT + AHEAD:
                                x_lo(b + 1, 1 - slot)
                    if last:
                        relu_lo(b, FT - 1)
                    else:
                        step(b, FT)
                    outputs(b)

                dve.memset(rstd[:, :], 0.0).then_inc(y_ready, NT)
                statistics(1)
                normalise(1)
                x_lo(0, 0)
                step(0, 0)
                over_batches(dve, batch)

        with ExitStack() as att:
            wqT = [sb(att, f"wqT{i}", [P, KT, D], F32R) for i in range(2)]
            woT = [sb(att, f"woT{i}", [P, KT, D], F32R) for i in range(2)]
            setup(att, wqT, woT)
            attention(att, wqT, woT)
        with ExitStack() as ff:
            w1_split = [sb(ff, f"w1_split{i}", [P, KT, F], F32R) for i in range(2)]
            w2_split = [sb(ff, f"w2_split{i}", [P, FT, D], F32R) for i in range(2)]
            turns_phase = sb(ff, "turns_phase", [P, FT])
            sine_gain = sb(ff, "sine_gain", [P, FT])
            b2_rows = sb(ff, "b2_rows", [P, D])
            with ExitStack() as st:
                ffn_setup(st, w1_split, w2_split, turns_phase, sine_gain, b2_rows)
            ffn(ff, w1_split, w2_split, turns_phase, sine_gain, b2_rows)


_INS = ['x', 'ctx_1024', 'g_xattn', 'g_ffn', 'L0_xattn_Wq', 'L0_xattn_bq', 'L0_xattn_Wk', 'L0_xattn_bk',
        'L0_xattn_Wv', 'L0_xattn_bv', 'L0_xattn_Wo', 'L0_xattn_bo', 'L0_ffn_W1', 'L0_ffn_b1',
        'L0_ffn_quantum_phases', 'L0_ffn_quantum_weights_real', 'L0_ffn_quantum_weights_imag', 'L0_ffn_W2',
        'L0_ffn_b2']
_OUTS = [((16, 512, 512), 'float32')]


def kernel(**inputs):
    import numpy as _np
    import concourse.bacc as _bacc
    from concourse import mybir as _mybir
    from concourse.bass_utils import run_bass_kernel_spmd as _run

    nc = _bacc.Bacc("TRN2", target_bir_lowering=False, num_devices=1)
    arrays, args = {}, []
    for name in _INS:
        a = _np.ascontiguousarray(inputs[name])
        arrays[f"in_{name}_dram"] = a
        args.append(nc.dram_tensor(f"in_{name}_dram", a.shape, _mybir.dt.from_np(a.dtype), kind="ExternalInput").ap())
    for i, (shape, dtype) in enumerate(_OUTS):
        dt = _mybir.dt.from_np(_np.dtype(dtype))
        args.append(nc.dram_tensor(f"out_{i}_dram", shape, dt, kind="ExternalOutput").ap())
    gated_attention_ffn_kernel(nc, *args)
    r = _run(nc, [arrays], core_ids=[0])
    got = tuple(r.results[0][f"out_{i}_dram"] for i in range(len(_OUTS)))
    return got[0]
```

```python
from contextlib import ExitStack

import concourse.bass as bass
from concourse import mybir

F32 = mybir.dt.float32
F32R = mybir.dt.float32r
ALU = mybir.AluOpType
ACT = mybir.ActivationFunctionType
AX_X = mybir.AxisListType.X

P = 128
HEADS = 16
EPS = 1e-5
TWO_PI = 6.283185307179586
TWO_PI_PARTS = (6.28125, 0.00193405151367187500, TWO_PI - 6.28125 - 0.00193405151367187500)
TWO_PI_BELOW = 6.2831850051879883
ROUND_MAGIC = 12582912.0

PASSES = ((0, 0), (0, 1), (1, 0))


def matmul3(pe, out, stationary, moving, first, last):
    for n, (s, m) in enumerate(PASSES):
        mm = pe.matmul(out, stationary(s), moving(m), start=first and n == 0,
                       stop=last and n == len(PASSES) - 1)
    return mm


class Count:

    def __init__(self, done, parity):
        self.done, self.parity, self.uses = done, parity % 2, 0

    def next(self):
        self.uses += 1
        return self.done + self.uses, (self.parity + self.uses - 1) % 2


class Slot:
    pass


def gated_attention_ffn_kernel(nc, x, ctx_in, g_xattn, g_ffn, wq, bq, wk, bk, wv, bv, wo, bo,
                               w1, b1, phases, w_real, w_imag, w2, b2, out):
    B, N, D = x.shape
    M = ctx_in.shape[1]
    F = w1.shape[1]
    DH = D // HEADS
    KT = D // P
    NT = N // P
    FT = F // P
    G = D // P
    HG = P // DH
    GC = HG * M
    PC = -(-2 * GC // P)
    NC = -(-GC // P)
    FROM = (0, GC - (NC - 1) * P)
    HALF = NT // 2
    UR = HALF * HG
    CB = 4
    ROUNDS = B // CB
    ROWS = CB * M
    RT = -(-ROWS // P)
    HT = 2
    CHUNK = HT * D
    CHUNKS = 2 * FT // HT
    STAGED = 3
    SCALE = float(DH) ** -0.5
    NVEC = 4 * FT + 2 * G
    assert N == 512 and D == 512 and G == KT == NT == 4 and B % CB == 0 and NC == 3 and PC == 5 and FT == 16

    x1 = nc.dram_tensor("x1_scratch", [B, N, D], F32).ap()
    k_parts = nc.dram_tensor("k_scratch", [B, G, P, 2, M], F32).ap()
    v_parts = nc.dram_tensor("v_scratch", [B * M, 2, D], F32).ap()

    ctx_rows = ctx_in.rearrange("b m d -> (b m) d")
    x_tiles = x.rearrange("b (t p) d -> b p t d", p=P)
    x1_tiles = x1.rearrange("b (t p) d -> b p t d", p=P)
    x1_rows = x1.rearrange("b (t p) d -> (b t) p d", p=P)
    out_rows = out.rearrange("b (t p) d -> (b t) p d", p=P)

    with ExitStack() as whole:
        def sb(stack, name, shape, dt=F32):
            return stack.enter_context(nc.sbuf_tensor(name, shape, dt))

        def sem(stack, name):
            return stack.enter_context(nc.semaphore(name))

        pair_bank = [whole.enter_context(nc.psum_tensor(f"pair_bank{i}", [P, 2, 512], F32)) for i in range(2)]
        t_bank = [whole.enter_context(nc.psum_tensor(f"t_bank{i}", [P, 512], F32)) for i in range(2)]
        m_bank = [whole.enter_context(nc.psum_tensor(f"m_bank{i}", [P, 512], F32)) for i in range(2)]

        ident = sb(whole, "ident", [P, P])
        minus_half = sb(whole, "minus_half", [P, NT])
        tanh_g = sb(whole, "tanh_g", [P, 2])
        columns = sb(whole, "columns", [P, NVEC])
        b1_col = columns[:, 0:FT]
        phase_col = columns[:, FT:2 * FT]
        real_col = columns[:, 2 * FT:3 * FT]
        imag_col = columns[:, 3 * FT:4 * FT]
        bq_col = columns[:, 4 * FT:4 * FT + G]
        bk_col = columns[:, 4 * FT + G:NVEC]

        turns_phase = sb(whole, "turns_phase", [P, FT])
        sine_gain = sb(whole, "sine_gain", [P, FT])

        x_in = sb(whole, "x_in", [P, NT, D])
        stats = sb(whole, "stats", [P, NT, 6])
        moments = sb(whole, "moments", [P, 3, NT])
        mean = sb(whole, "mean", [P, NT])
        var_eps = sb(whole, "var_eps", [P, NT])
        rstd = sb(whole, "rstd", [P, NT])
        xT = [[sb(whole, f"xT{s}_{i}", [P, KT, N], F32R) for i in range(2)] for s in range(2)]
        x_loaded = sem(whole, "x_loaded")
        stats_ready = sem(whole, "stats_ready")
        sums_ready = sem(whole, "sums_ready")
        mean_ready = sem(whole, "mean_ready")
        var_ready = sem(whole, "var_ready")
        rstd_ready = sem(whole, "rstd_ready")
        normed = sem(whole, "normed")

        def sums(dve, n, tiles=range(NT)):
            dve.wait_ge(x_loaded, 16 * n)
            for tile in tiles:
                dve.bn_stats(stats[:, tile, :], x_in[:, tile, :]).then_inc(stats_ready, 1)

        def statistics(dve, n):
            dve.wait_ge(stats_ready, NT * n)
            dve.tensor_tensor(moments[:, 0, :], stats[:, :, 1], stats[:, :, 4], ALU.add)
            dve.tensor_tensor(moments[:, 1, :], stats[:, :, 1], stats[:, :, 4], ALU.subtract)
            dve.tensor_tensor(moments[:, 2, :], stats[:, :, 2], stats[:, :, 5], ALU.add).then_inc(sums_ready, 1)
            dve.wait_ge(sums_ready, n)
            dve.tensor_scalar(mean[:, :], moments[:, 0, :], 0.5, None, ALU.mult)
            dve.scalar_tensor_tensor(out=moments[:, 1, :], in0=moments[:, 1, :], scalar=0.25,
                                     in1=moments[:, 1, :], op0=ALU.mult, op1=ALU.mult)
            dve.tensor_scalar(moments[:, 2, :], moments[:, 2, :], 1.0 / D, EPS, ALU.mult, ALU.add)\
               .then_inc(mean_ready, 1)
            dve.wait_ge(mean_ready, n)
            dve.tensor_tensor(var_eps[:, :], moments[:, 1, :], moments[:, 2, :], ALU.add).then_inc(var_ready, 1)

        def rstd_of(pool, n):
            pool.wait_ge(var_ready, n)
            pool.tensor_tensor(rstd[:, :], var_eps[:, :], minus_half[:, :], ALU.pow).then_inc(rstd_ready, 1)

        def normalise(dve, n):
            dve.wait_ge(rstd_ready, n)
            for tile in range(NT):
                dve.tensor_scalar(x_in[:, tile, :], x_in[:, tile, :], mean[:, tile:tile + 1],
                                  rstd[:, tile:tile + 1], ALU.subtract, ALU.mult).then_inc(normed, 1)

        residual = [sb(whole, f"residual{t}", [P, D]) for t in range(NT)]
        x1_stored = [sem(whole, f"x1_stored{t}") for t in range(NT)]

        w_chunk = [sb(whole, f"w_chunk{i}", [P, CHUNK]) for i in range(STAGED)]
        chunk_loaded = [sem(whole, f"chunk_loaded{i}") for i in range(STAGED)]
        w1_number = [0] + [2 * g - 1 for g in range(1, FT // HT)]
        w2_number = [2 * g + 2 for g in range(FT // HT - 1)] + [CHUNKS - 1]

        def load_chunk(sp, n):
            to = w_chunk[n % STAGED]
            if n in w1_number:
                g = w1_number.index(n)
                sp.dma_start(to[:, :].rearrange("p (k f) -> p k f", k=KT),
                             w1.rearrange("(k p) f -> p k f", p=P)[:, :, HT * P * g:HT * P * (g + 1)])\
                  .then_inc(chunk_loaded[n % STAGED], 16)
            else:
                g = w2_number.index(n)
                sp.dma_start(to[:, :].rearrange("p (f d) -> p f d", f=HT),
                             w2.rearrange("(f p) d -> p f d", p=P)[:, HT * g:HT * (g + 1)])\
                  .then_inc(chunk_loaded[n % STAGED], 16)

        att = whole.enter_context(ExitStack())
        wqT = [sb(att, f"wqT{i}", [P, KT, D], F32R) for i in range(2)]
        woT = [sb(att, f"woT{i}", [P, KT, D], F32R) for i in range(2)]
        qT = [[sb(att, f"qT{s}_{i}", [P, N], F32R) for i in range(2)] for s in range(2)]
        k_diag = sb(att, "k_diag", [P, G, 2, GC], F32R)
        v_diag = sb(att, "v_diag", [P, G, 2, NC, P], F32R)
        cleared = sem(whole, "cleared")
        keys_loaded = [sem(whole, f"keys_loaded{g}") for g in range(G)]
        values_loaded = [sem(whole, f"values_loaded{g}") for g in range(G)]
        first_keys_loaded = sem(whole, "first_keys_loaded")
        first_values_loaded = sem(whole, "first_values_loaded")
        pieces = [[], []]
        for second in range(2):
            for j in range(HG):
                r = FROM[second] + j * M
                end = r + M
                while r < end:
                    n = min(end, (r // P + 1) * P) - r
                    pieces[second].append((j, r // P, r % P, M - (end - r), n))
                    r += n
        assert len(pieces[0]) == len(pieces[1])
        PIECES = len(pieces[0])

        def load_keys(queue, b, g, loaded):
            for j in range(HG):
                rows = slice(j * DH, (j + 1) * DH)
                queue.dma_start(k_diag[rows, g, :, j * M:(j + 1) * M].bitcast(F32), k_parts[b, g, rows])\
                  .then_inc(loaded, 16)

        def load_values(queue, b, g, loaded):
            for j, c, p0, m0, n in pieces[g % 2]:
                cols = slice(g * P + j * DH, g * P + (j + 1) * DH)
                queue.dma_start(v_diag[p0:p0 + n, g, :, c, j * DH:(j + 1) * DH].bitcast(F32),
                                v_parts[bass.ds(M * b + m0, n), :, cols]).then_inc(loaded, 16)

        def setup():
            with ExitStack() as st:
                wkT, wvT = xT
                w_raw = [sb(st, f"w_raw{i}", [P, KT, D]) for i in range(4)]
                vector_rows = sb(st, "vector_rows", [NVEC, P])
                g_raw = sb(st, "g_raw", [P, 2])
                bv_rows = sb(st, "bv_rows", [P, D])
                ctx_raw = sb(st, "ctx_raw", [P, RT, D])
                ctxT = [sb(st, f"ctxT{i}", [P, KT, ROWS], F32R) for i in range(2)]
                kT = sb(st, "kT", [P, G, CB, 2, M], F32R)
                v_sum = [sb(st, f"v_sum{j}", [P, D]) for j in range(RT)]
                v_pair = [sb(st, f"v_pair{j}", [P, 2, D], F32R) for j in range(RT)]
                work = [sb(st, f"phase_work{i}", [P, FT]) for i in range(4)]

                wk_loaded = [sem(st, f"wk_loaded{kt}") for kt in range(KT)]
                weights_loaded = [None] + [sem(st, f"weights_loaded{i}") for i in range(1, 4)]
                vectors_loaded = sem(st, "vectors_loaded")
                bv_loaded = sem(st, "bv_loaded")
                ctx_loaded = sem(st, "ctx_loaded")
                zeroed = sem(st, "zeroed")
                ident_ready = sem(st, "ident_ready")
                phase_step = sem(st, "phase_step")
                sines_ready = sem(st, "sines_ready")
                t_full = sem(st, "t_full_s")
                t_hi = sem(st, "t_hi_s")
                t_split = sem(st, "t_split_s")
                proj_full = sem(st, "proj_full")
                proj_hi = sem(st, "proj_hi")
                proj_split = sem(st, "proj_split")
                v_full = sem(st, "v_full")
                v_summed = sem(st, "v_summed")
                v_hi = sem(st, "v_hi")
                v_split = sem(st, "v_split")
                k_stored = [sem(st, f"k_stored{g}") for g in range(G)]
                v_stored = [sem(st, f"v_stored{j}") for j in range(RT)]

                s_bank = [t_bank[0], t_bank[1], pair_bank[1][:, 0, :], pair_bank[1][:, 1, :]]
                v_bank = [pair_bank[0][:, j, :] for j in range(2)]

                WK_AT, CTX0_AT, VECTORS_AT = (KT * i for i in range(3))
                WV_AT, WQ_AT = (VECTORS_AT + 1 + KT * i for i in range(2))

                def ctx_at(r):
                    return 1 + KT * 3 + KT * r

                X_AT = ctx_at(ROUNDS)
                WO_AT = X_AT + KT

                def ctx_bank(at, kt):
                    return s_bank[(kt + (0 if at is CTX0_AT else 1)) % 4]

                def hi_number(t):
                    return t + 1 if isinstance(t, int) and t < VECTORS_AT else t

                def v_rows(j):
                    return min(P, ROWS - P * j)

                block = st.enter_context(nc.Block())

                @block.sync
                def _(sp):
                    def load_weight(i, w):
                        sp.dma_start(w_raw[i][:, :, :], w.rearrange("(t p) k -> p t k", p=P))\
                          .then_inc(weights_loaded[i], 16)

                    def load_context(r):
                        for j in range(RT):
                            sp.dma_start(ctx_raw[0:v_rows(j), j, :], ctx_rows[bass.ds(ROWS * r + P * j, v_rows(j))])\
                              .then_inc(ctx_loaded, 16)

                    def store_keys(r):
                        for g in range(G):
                            sp.wait_ge(proj_split, G * r + g + 1)
                            sp.dma_start(k_parts[bass.ds(CB * r, CB), g].rearrange("b p t m -> p b t m"),
                                         kT[:, g, :, :, :].bitcast(F32)).then_inc(k_stored[g], 16)

                    def store_values(r):
                        for j in range(RT):
                            sp.wait_ge(v_split, RT * r + j + 1)
                            sp.dma_start(v_parts[bass.ds(ROWS * r + P * j, v_rows(j))],
                                         v_pair[j][0:v_rows(j), :, :].bitcast(F32)).then_inc(v_stored[j], 16)

                    for kt in range(KT):
                        sp.dma_start(w_raw[0][:, :, kt * P:(kt + 1) * P],
                                     wk.rearrange("(t p) k -> p t k", p=P)[:, :, kt * P:(kt + 1) * P])\
                          .then_inc(wk_loaded[kt], 16)
                    load_context(0)
                    load_weight(1, wv)
                    sp.dma_start(x_in[:, :, :], x_tiles[0]).then_inc(x_loaded, 16)
                    load_weight(2, wq)
                    sp.dma_start(bv_rows[:, :], bv.rearrange("(a d) -> a d", a=1).to_broadcast([P, D]))\
                      .then_inc(bv_loaded, 16)
                    load_weight(3, wo)
                    sp.wait_ge(t_full, CTX0_AT + KT)
                    load_context(1)
                    store_keys(0)
                    store_values(0)
                    with sp.Fori(1, ROUNDS - 1) as r:
                        sp.wait_ge(t_full, ctx_at(r) + KT)
                        load_context(r + 1)
                        store_keys(r)
                        store_values(r)
                    store_keys(ROUNDS - 1)
                    sp.wait_ge(t_full, X_AT + KT)
                    sp.dma_start(x_in[:, :, :], x_tiles[1]).then_inc(x_loaded, 16)
                    store_values(ROUNDS - 1)
                    for stored in k_stored + v_stored:
                        sp.wait_ge(stored, 16 * ROUNDS)

                @block.gpsimd
                def _(pool):
                    pool.memset(minus_half[:, :], -0.5)
                    pool.memset(ident[:, :], 0.0).then_inc(zeroed, 1)
                    pool.wait_ge(zeroed, 1)
                    pool.affine_select(out=ident[:, :], in_=ident[:, :], compare_op=ALU.not_equal, fill=1.0,
                                       base=0, pattern=[[-1, P]], channel_multiplier=1).then_inc(ident_ready, 1)
                    pool.memset(k_diag[:, :, :, :].bitcast(F32), 0.0)
                    pool.memset(v_diag[:, :, :, :, :].bitcast(F32), 0.0).then_inc(cleared, 1)
                    rstd_of(pool, 1)
                    pool.wait_ge(cleared, 1)
                    for g in range(G):
                        pool.wait_ge(k_stored[g], 16)
                        load_keys(pool, 0, g, first_keys_loaded)
                    for j in range(RT):
                        pool.wait_ge(v_stored[j], 16)
                    for g in range(G):
                        load_values(pool, 0, g, first_values_loaded)

                @block.tensor
                def _(pe):
                    def transpose_weight(i, at):
                        for kt in range(KT):
                            if i == 0:
                                pe.wait_ge(wk_loaded[kt], 16)
                            elif kt == 0:
                                pe.wait_ge(weights_loaded[i], 16)
                            t = at + kt
                            if t > 3:
                                pe.wait_ge(t_split, t - 3)
                            for ot in range(KT):
                                tr = pe.transpose(s_bank[t % 4][:, ot * P:(ot + 1) * P],
                                                  w_raw[i][:, ot, kt * P:(kt + 1) * P], ident[:, :])
                            tr.then_inc(t_full, 1)

                    def transpose_context(r, at):
                        pe.wait_ge(ctx_loaded, 16 * RT * (r + 1))
                        for kt in range(KT):
                            pe.wait_ge(t_split, at + kt - 3)
                            for j in range(RT):
                                n = v_rows(j)
                                tr = pe.transpose(ctx_bank(at, kt)[:, P * j:P * j + n],
                                                  ctx_raw[0:n, j, kt * P:(kt + 1) * P], ident[0:n, 0:n])
                            tr.then_inc(t_full, 1)

                    def keys(r, at):
                        for g in range(G):
                            if not (isinstance(r, int) and r == 0 and g < 2):
                                pe.wait_ge(proj_split, G * r + g - 1)
                            for kt in range(KT):
                                if g == 0:
                                    pe.wait_ge(t_split, at + kt + 1)
                                mm = matmul3(pe, m_bank[g % 2][:, 0:ROWS],
                                             lambda p: wkT[p][:, kt, g * P:(g + 1) * P],
                                             lambda p: ctxT[p][:, kt, :], kt == 0, kt == KT - 1)
                            mm.then_inc(proj_full, 1)

                    def values(r):
                        for j in range(RT):
                            if isinstance(r, int) and r == 0:
                                if j == 0:
                                    pe.wait_ge(t_split, WV_AT + KT)
                            elif j == 0:
                                pe.wait_ge(v_summed, RT * r)
                            if j == 2:
                                pe.wait_ge(v_summed, RT * r + 1)
                            n = v_rows(j)
                            for kt in range(KT):
                                mm = matmul3(pe, v_bank[j % 2][0:n, :],
                                             lambda p: ctxT[p][:, kt, P * j:P * j + n],
                                             lambda p: wvT[p][:, kt, :], kt == 0, kt == KT - 1)
                            mm.then_inc(v_full, 1)

                    pe.wait_ge(ident_ready, 1)
                    transpose_weight(0, WK_AT)
                    transpose_context(0, CTX0_AT)
                    pe.wait_ge(vectors_loaded, 16 * 8)
                    pe.wait_ge(t_split, VECTORS_AT - 3)
                    pe.transpose(s_bank[VECTORS_AT % 4][:, 0:NVEC], vector_rows[:, :], ident[0:NVEC, 0:NVEC])\
                      .then_inc(t_full, 1)
                    keys(0, CTX0_AT)
                    transpose_weight(1, WV_AT)
                    transpose_weight(2, WQ_AT)
                    values(0)
                    transpose_context(1, ctx_at(1))
                    with pe.Fori(1, ROUNDS - 1) as r:
                        keys(r, ctx_at(r))
                        values(r)
                        transpose_context(r + 1, ctx_at(r + 1))
                    keys(ROUNDS - 1, ctx_at(ROUNDS - 1))
                    pe.wait_ge(normed, NT)
                    for kt in range(KT):
                        pe.wait_ge(t_split, X_AT + kt - 3)
                        for tile in range(NT):
                            tr = pe.transpose(s_bank[(X_AT + kt) % 4][:, tile * P:(tile + 1) * P],
                                              x_in[:, tile, kt * P:(kt + 1) * P], ident[:, :])
                        tr.then_inc(t_full, 1)
                    transpose_weight(3, WO_AT)
                    values(ROUNDS - 1)
                    pe.wait_ge(t_split, X_AT + KT)
                    pe.wait_ge(proj_split, G * ROUNDS - 1)
                    for kt in range(KT):
                        mm = matmul3(pe, m_bank[0][:, :], lambda p: wqT[p][:, kt, 0:P],
                                     lambda p: xT[0][p][:, kt, :], kt == 0, kt == KT - 1)
                    mm.then_inc(proj_full, 1)

                @block.scalar
                def _(act):
                    def weight_hi(parts, at):
                        for kt in range(KT):
                            act.wait_ge(t_full, at + kt + 1)
                            act.activation(parts[0][:, kt, :], s_bank[(at + kt) % 4][:, :], ACT.Copy).then_inc(t_hi, 1)

                    def context_hi(at, kts=range(KT)):
                        for kt in kts:
                            act.wait_ge(t_full, at + kt + 1)
                            act.activation(ctxT[0][:, kt, :], ctx_bank(at, kt)[:, 0:ROWS], ACT.Copy).then_inc(t_hi, 1)

                    def keys_hi(r):
                        for g in range(G):
                            act.wait_ge(proj_full, G * r + g + 1)
                            if not (isinstance(r, int) and r == 0):
                                act.wait_ge(k_stored[g], 16 * r)
                            act.activation(kT[:, g, :, 0, :], m_bank[g % 2][:, 0:ROWS].rearrange("p (b m) -> p b m", m=M),
                                           ACT.Identity, bias=bk_col[:, g:g + 1]).then_inc(proj_hi, 1)

                    def values_hi(r, j):
                        act.wait_ge(v_summed, RT * r + j + 1)
                        if not (isinstance(r, int) and r == 0):
                            act.wait_ge(v_stored[j], 16 * r)
                        n = v_rows(j)
                        act.activation(v_pair[j][0:n, 0, :], v_sum[j][0:n, :], ACT.Copy).then_inc(v_hi, 1)

                    row = 0
                    for vec in (b1, phases, w_real, w_imag, bq, bk):
                        rows = vec.rearrange("(t p) -> t p", p=P)
                        act.dma_start(vector_rows[row:row + rows.shape[0], :], rows).then_inc(vectors_loaded, 16)
                        row += rows.shape[0]
                    for i, g in enumerate((g_xattn, g_ffn)):
                        act.dma_start(g_raw[:, i:i + 1], g.rearrange("(a b) -> a b", b=1).to_broadcast([P, 1]))\
                           .then_inc(vectors_loaded, 16)
                    weight_hi(wkT, WK_AT)
                    context_hi(CTX0_AT)
                    act.wait_ge(t_split, VECTORS_AT + 1)
                    keys_hi(0)
                    weight_hi(wvT, WV_AT)
                    weight_hi(wqT, WQ_AT)
                    act.wait_ge(vectors_loaded, 16 * 8)
                    act.activation(tanh_g[:, :], g_raw[:, :], ACT.Tanh)
                    act.wait_ge(phase_step, 9)
                    act.activation(work[2][:, :], turns_phase[:, :], ACT.Sin, scale=TWO_PI_BELOW)
                    act.activation(work[3][:, :], work[1][:, :], ACT.Sin, scale=TWO_PI_BELOW).then_inc(sines_ready, 1)
                    for j in range(RT - 1):
                        values_hi(0, j)
                    context_hi(ctx_at(1), (0, 1))
                    values_hi(0, RT - 1)
                    context_hi(ctx_at(1), (2, 3))
                    with act.Fori(1, ROUNDS - 1) as r:
                        keys_hi(r)
                        for j in range(RT - 1):
                            values_hi(r, j)
                        context_hi(ctx_at(r + 1), (0, 1))
                        values_hi(r, RT - 1)
                        context_hi(ctx_at(r + 1), (2, 3))
                    keys_hi(ROUNDS - 1)
                    for kt in range(KT):
                        act.wait_ge(t_full, X_AT + kt + 1)
                        act.activation(xT[0][0][:, kt, :], s_bank[(X_AT + kt) % 4][:, :], ACT.Copy).then_inc(t_hi, 1)
                    weight_hi(woT, WO_AT)
                    for j in range(RT):
                        values_hi(ROUNDS - 1, j)
                    act.wait_ge(proj_full, G * ROUNDS + 1)
                    act.activation(qT[0][0][:, :], m_bank[0][:, :], ACT.Identity, bias=bq_col[:, 0:1])\
                       .then_inc(proj_hi, 1)

                @block.vector
                def _(dve):
                    def weight_lo(parts, at):
                        for kt in range(KT):
                            dve.wait_ge(t_hi, hi_number(at + kt))
                            dve.tensor_tensor(parts[1][:, kt, :], s_bank[(at + kt) % 4][:, :],
                                              parts[0][:, kt, :].bitcast(F32), ALU.subtract).then_inc(t_split, 1)

                    def context_lo(at, kts=range(KT)):
                        for kt in kts:
                            dve.wait_ge(t_hi, hi_number(at + kt))
                            dve.tensor_tensor(ctxT[1][:, kt, :], ctx_bank(at, kt)[:, 0:ROWS],
                                              ctxT[0][:, kt, :].bitcast(F32), ALU.subtract).then_inc(t_split, 1)

                    def keys_lo(r, gs=range(G)):
                        for g in gs:
                            dve.wait_ge(proj_hi, G * r + g + 1)
                            dve.scalar_tensor_tensor(out=kT[:, g, :, 1, :],
                                                     in0=m_bank[g % 2][:, 0:ROWS].rearrange("p (b m) -> p b m", m=M),
                                                     scalar=bk_col[:, g:g + 1], in1=kT[:, g, :, 0, :].bitcast(F32),
                                                     op0=ALU.add, op1=ALU.subtract).then_inc(proj_split, 1)

                    def values_sum(r, j):
                        n = v_rows(j)
                        dve.wait_ge(v_full, RT * r + j + 1)
                        dve.tensor_tensor(v_sum[j][0:n, :], v_bank[j % 2][0:n, :], bv_rows[0:n, :], ALU.add)\
                           .then_inc(v_summed, 1)

                    def values_lo(r, j):
                        n = v_rows(j)
                        dve.wait_ge(v_hi, RT * r + j + 1)
                        dve.tensor_tensor(v_pair[j][0:n, 1, :], v_sum[j][0:n, :], v_pair[j][0:n, 0, :].bitcast(F32),
                                          ALU.subtract).then_inc(v_split, 1)

                    steps = [0]

                    def stepped(instruction):
                        steps[0] += 1
                        instruction.then_inc(phase_step, 1)
                        dve.wait_ge(phase_step, steps[0])

                    def phases_in_turns():
                        stepped(dve.tensor_scalar(work[0][:, :], phase_col, 1.0 / TWO_PI, ROUND_MAGIC, ALU.mult, ALU.add))
                        stepped(dve.tensor_scalar(work[0][:, :], work[0][:, :], ROUND_MAGIC, None, ALU.subtract))
                        stepped(dve.scalar_tensor_tensor(out=work[1][:, :], in0=work[0][:, :], scalar=-TWO_PI_PARTS[0],
                                                         in1=phase_col, op0=ALU.mult, op1=ALU.add))
                        stepped(dve.scalar_tensor_tensor(out=work[1][:, :], in0=work[0][:, :], scalar=-TWO_PI_PARTS[1],
                                                         in1=work[1][:, :], op0=ALU.mult, op1=ALU.add))
                        stepped(dve.scalar_tensor_tensor(out=work[1][:, :], in0=work[0][:, :], scalar=-TWO_PI_PARTS[2],
                                                         in1=work[1][:, :], op0=ALU.mult, op1=ALU.add))
                        stepped(dve.tensor_scalar(work[1][:, :], work[1][:, :], 1.0 / TWO_PI, 0.5, ALU.mult, ALU.min))
                        stepped(dve.tensor_scalar(turns_phase[:, :], work[1][:, :], -0.5, None, ALU.max))
                        stepped(dve.tensor_scalar(work[0][:, :], turns_phase[:, :], 0.25, -1.0, ALU.is_gt, ALU.mult))
                        stepped(dve.scalar_tensor_tensor(out=work[1][:, :], in0=turns_phase[:, :], scalar=0.25,
                                                         in1=work[0][:, :], op0=ALU.add, op1=ALU.add))

                    def hidden_constants():
                        dve.wait_ge(sines_ready, 1)
                        stepped(dve.scalar_tensor_tensor(out=turns_phase[:, :], in0=b1_col, scalar=0.1 / TWO_PI,
                                                         in1=turns_phase[:, :], op0=ALU.mult, op1=ALU.add))
                        stepped(dve.tensor_tensor(work[3][:, :], work[3][:, :], real_col, ALU.mult))
                        stepped(dve.tensor_tensor(work[2][:, :], work[2][:, :], imag_col, ALU.mult))
                        stepped(dve.tensor_tensor(work[3][:, :], work[3][:, :], work[2][:, :], ALU.add))
                        stepped(dve.scalar_tensor_tensor(out=sine_gain[:, :], in0=work[3][:, :], scalar=0.1,
                                                         in1=imag_col, op0=ALU.mult, op1=ALU.mult))

                    weight_lo(wkT, WK_AT)
                    context_lo(CTX0_AT)
                    dve.wait_ge(t_full, VECTORS_AT + 1)
                    dve.tensor_copy(columns[:, :], s_bank[VECTORS_AT % 4][:, 0:NVEC]).then_inc(t_split, 1)
                    dve.wait_ge(t_split, VECTORS_AT + 1)
                    phases_in_turns()
                    for g in range(G):
                        keys_lo(0, (g,))
                        sums(dve, 1, (g,))
                    weight_lo(wvT, WV_AT)
                    weight_lo(wqT, WQ_AT)
                    statistics(dve, 1)
                    dve.wait_ge(bv_loaded, 16)
                    for j in range(RT - 1):
                        values_sum(0, j)
                        values_lo(0, j)
                    values_sum(0, RT - 1)
                    context_lo(ctx_at(1), (0, 1))
                    values_lo(0, RT - 1)
                    context_lo(ctx_at(1), (2, 3))
                    with dve.Fori(1, ROUNDS - 1) as r:
                        keys_lo(r)
                        for j in range(RT - 1):
                            values_sum(r, j)
                            values_lo(r, j)
                        values_sum(r, RT - 1)
                        context_lo(ctx_at(r + 1), (0, 1))
                        values_lo(r, RT - 1)
                        context_lo(ctx_at(r + 1), (2, 3))
                    normalise(dve, 1)
                    keys_lo(ROUNDS - 1)
                    for kt in range(KT):
                        dve.wait_ge(t_hi, X_AT + kt)
                        dve.tensor_tensor(xT[0][1][:, kt, :], s_bank[(X_AT + kt) % 4][:, :],
                                          xT[0][0][:, kt, :].bitcast(F32), ALU.subtract).then_inc(t_split, 1)
                    weight_lo(woT, WO_AT)
                    for j in range(RT):
                        values_sum(ROUNDS - 1, j)
                        values_lo(ROUNDS - 1, j)
                    dve.wait_ge(proj_hi, G * ROUNDS + 1)
                    dve.scalar_tensor_tensor(out=qT[0][1][:, :], in0=m_bank[0][:, :], scalar=bq_col[:, 0:1],
                                             in1=qT[0][0][:, :].bitcast(F32), op0=ALU.add, op1=ALU.subtract)\
                       .then_inc(proj_split, 1)
                    hidden_constants()

        def attention(st):
            peak = [sb(st, f"peak{i}", [P, UR]) for i in range(2)]
            exp_bias = [sb(st, f"exp_bias{i}", [P, UR]) for i in range(2)]
            exp_sum = [sb(st, f"exp_sum{i}", [P, UR]) for i in range(2)]
            exp_inv = [sb(st, f"exp_inv{i}", [P, UR]) for i in range(2)]
            exps = [sb(st, f"exps{i}", [P, HALF, GC]) for i in range(2)]
            probs = [sb(st, f"probs{i}", [P, NT, PC * P]) for i in range(G // 2)]
            probsT = [sb(st, f"probsT{i}", [P, PC, N], F32R) for i in range(2)]
            oT = [[sb(st, f"oT{s}_{i}", [P, G, N], F32R) for i in range(2)] for s in range(2)]
            bo_rows = sb(st, "bo_rows", [P, D])

            t_full = sem(st, "t_full_a")
            t_hi = sem(st, "t_hi_a")
            t_split = sem(st, "t_split_a")
            m_full = sem(st, "m_full_a")
            m_hi = sem(st, "m_hi_a")
            m_split = sem(st, "m_split_a")
            scores_full = sem(st, "scores_full")
            peak_ready = sem(st, "peak_ready")
            bias_ready = sem(st, "bias_ready")
            exps_ready = sem(st, "exps_ready")
            inv_ready = sem(st, "inv_ready")
            probs_ready = sem(st, "probs_ready")
            bo_loaded = sem(st, "bo_loaded")
            bo_gated = sem(st, "bo_gated")
            residual_loaded = [sem(st, f"residual_loaded{t}") for t in range(NT)]
            residual_ready = sem(st, "residual_ready")

            FIRST, SECOND, MIDDLE, LAST, AFTER = range(5)

            def slots_of(b, place):
                if place == FIRST:
                    t, m, h = Count(0, 0), Count(0, 0), Count(0, 0)
                else:
                    t_less = PC
                    m_less = 2 + (G if place == SECOND else G + 2) + (1 if place == AFTER else 0)
                    h_less = 2 + (1 if place == AFTER else 0)
                    t = Count(b * (2 * PC + KT) - t_less, t_less)
                    m = Count(b * (3 * G) - m_less, m_less)
                    h = Count(b * (2 * G) - h_less, 0)
                queries_done = m.done - {FIRST: 0, SECOND: 1}.get(place, 2 if place != AFTER else 1)
                slots = []
                for g in range(G if place != AFTER else 2):
                    s = Slot()
                    s.queries_done = queries_done
                    s.finish = place != FIRST if g < 2 else place != AFTER
                    s.score = place != AFTER
                    s.back = (b - 1, g + 2) if g < 2 else (b, g - 2)
                    s.output = None
                    s.chunks = range(NC) if g % 2 == 0 else range(NC, PC)
                    s.probs = {c: t.next() for c in s.chunks} if s.finish else None
                    s.x = [t.next() for _ in range(2)] if g in (1, 2) and place != AFTER else None
                    s.queries = None
                    s.values_first = place == AFTER and g == 1
                    if s.values_first:
                        s.values = (*m.next(), h.next()[0])
                    if s.score and not (place == LAST and g == G - 1):
                        s.queries = (*m.next(), h.next()[0])
                        queries_done = s.queries[0]
                    if g >= 2 and place != FIRST:
                        s.output = (b - 1, g - 2, *m.next())
                    if g < 2 and place not in (FIRST, SECOND):
                        s.output = (b - 2, g + 2, *m.next())
                    if not s.values_first:
                        s.values = (*m.next(), h.next()[0]) if s.finish else None
                    slots.append(s)
                return slots

            def outputs_after():
                m_less = 2 + G + 2 + 1
                m = Count(B * 3 * G - m_less + 2 * 2, m_less)
                return [(tile, *m.next()) for tile in range(NT)]

            def over_batches(eng, turn):
                turn(0, 0, FIRST)
                turn(1, 1, SECOND)
                with eng.Fori(2, B - 3, 2) as b:
                    turn(b, 0, MIDDLE)
                    turn(b + 1, 1, MIDDLE)
                turn(B - 2, 0, MIDDLE)
                turn(B - 1, 1, LAST)
                turn(B, 0, AFTER)

            def scores_view(half):
                return pair_bank[half][:, :, 0:GC].rearrange("p n (h m) -> p n h m", m=M)

            block = st.enter_context(nc.Block())

            @block.sync
            def _(sp):
                def load_x(source):
                    sp.dma_start(x_in[:, :, :], source).then_inc(x_loaded, 16)

                def load_residual(b, tile):
                    sp.dma_start(residual[tile][:, :], x_tiles[b, :, tile]).then_inc(residual_loaded[tile], 16)

                def reload_residual(b, tile):
                    sp.wait_ge(x1_stored[tile], 16 * b)
                    load_residual(b, tile)

                def store_y(b, tile, n):
                    sp.wait_ge(m_split, n)
                    sp.dma_start(x1_rows[NT * b + tile], residual[tile][:, :]).then_inc(x1_stored[tile], 16)

                def turn(b, parity, place):
                    for g, s in enumerate(slots_of(b, place)):
                        if g == 3 and place != FIRST:
                            reload_residual(b, 0)
                        if g < 3 and place not in (FIRST, SECOND):
                            reload_residual(b - 1, g + 1)
                        if place not in (LAST, AFTER):
                            sp.wait_ge(scores_full, 2 * G * b + 2 * g + 2)
                            load_keys(sp, b + 1, g, keys_loaded[g])
                        if g == 2 and place != AFTER:
                            sp.wait_ge(t_full, s.x[1][0])
                            if isinstance(b, int) and b + 2 >= B:
                                load_x(x1_tiles[b + 2 - B])
                            else:
                                load_x(x_tiles[b + 2])
                        if s.output:
                            store_y(s.output[0], s.output[1], s.output[2])
                        if s.finish and place != AFTER and not (place == LAST and g >= 2):
                            sp.wait_ge(m_full, s.values[0])
                            load_values(sp, s.back[0] + 1, s.back[1], values_loaded[s.back[1]])

                sp.dma_start(bo_rows[:, :], bo.rearrange("(a d) -> a d", a=1).to_broadcast([P, D])).then_inc(bo_loaded, 16)
                for tile in range(NT):
                    load_residual(0, tile)
                for n in range(STAGED):
                    load_chunk(sp, n)
                over_batches(sp, turn)
                reload_residual(B - 1, 3)
                for tile, n, _ in outputs_after():
                    store_y(B - 1, tile, n)

            @block.gpsimd
            def _(pool):
                pool.wait_ge(bo_loaded, 16)
                pool.tensor_scalar(bo_rows[:, :], bo_rows[:, :], tanh_g[:, 0:1], 0.0, ALU.mult, ALU.add)\
                    .then_inc(bo_gated, 1)

                def probabilities(unit, g, half):
                    pool.wait_ge(inv_ready, unit)
                    pool.tensor_tensor(
                        probs[g // 2][:, HALF * half:HALF * (half + 1), g % 2 * GC:(g % 2 + 1) * GC]
                        .rearrange("p n (h m) -> p n h m", m=M),
                        exps[half][:, :, :].rearrange("p n (h m) -> p n h m", m=M),
                        exp_inv[half][:, :].rearrange("p (n h o) -> p n h o", h=HG, o=1).to_broadcast([P, HALF, HG, M]),
                        ALU.mult).then_inc(probs_ready, 1)

                def add_bias(b, tile):
                    pool.wait_ge(residual_loaded[tile], 16 * (b + 1))
                    if isinstance(b, int) and b == 0 and tile == 0:
                        pool.wait_ge(bo_gated, 1)
                    pool.tensor_tensor(residual[tile][:, :], residual[tile][:, :], bo_rows[:, :], ALU.add)\
                        .then_inc(residual_ready, 1)

                def turn(b, parity, place):
                    for g, s in enumerate(slots_of(b, place)):
                        if place != FIRST:
                            add_bias(b - 1, g)
                        if s.score:
                            probabilities(2 * G * b + 2 * g + 1, g, 0)
                        if g == 0 and place != AFTER:
                            rstd_of(pool, b + 2)
                        if s.score:
                            probabilities(2 * G * b + 2 * g + 2, g, 1)

                for i in range(G // 2):
                    pool.memset(probs[i][:, :, 2 * GC:PC * P], 0.0)
                over_batches(pool, turn)
                for tile in (2, 3):
                    add_bias(B - 1, tile)

            @block.tensor
            def _(pe):
                def transpose_x(kt, n, bank, b):
                    if kt == 0:
                        pe.wait_ge(normed, NT * (b + 1))
                    if not (isinstance(n, int) and n <= 2):
                        pe.wait_ge(t_split, n - 2)
                    for tile in range(NT):
                        tr = pe.transpose(t_bank[bank][:, tile * P:(tile + 1) * P],
                                          x_in[:, tile, kt * P:(kt + 1) * P], ident[:, :])
                    tr.then_inc(t_full, 1)

                def transpose_probs(b, g, c, n, bank):
                    if c in (0, NC - 1):
                        pe.wait_ge(probs_ready, 2 * G * b + 2 * (g + (c == NC - 1)) + 2)
                    if not (isinstance(n, int) and n <= 2):
                        pe.wait_ge(t_split, n - 2)
                    for tile in range(NT):
                        tr = pe.transpose(t_bank[bank][:, tile * P:(tile + 1) * P],
                                          probs[g // 2][:, tile, c * P:(c + 1) * P], ident[:, :])
                    tr.then_inc(t_full, 1)

                def queries(parity, g, n, bank):
                    if not (isinstance(n, int) and n <= 2):
                        pe.wait_ge(m_split, n - 2)
                    for kt in range(KT):
                        mm = matmul3(pe, m_bank[bank][:, :], lambda p: wqT[p][:, kt, g * P:(g + 1) * P],
                                     lambda p: xT[parity][p][:, kt, :], kt == 0, kt == KT - 1)
                    mm.then_inc(m_full, 1)

                def scores(b, g, half, queries_done, first):
                    if half == 0:
                        if not (first and g == 0):
                            pe.wait_ge(m_split, queries_done)
                        if first:
                            pe.wait_ge(first_keys_loaded, 16 * HG * G)
                        else:
                            pe.wait_ge(keys_loaded[g], 16 * HG * b)
                    if not (first and g == 0):
                        pe.wait_ge(exps_ready, 2 * G * b + 2 * g + half - 1)
                    for n in range(HALF):
                        tile = HALF * half + n
                        mm = matmul3(pe, pair_bank[half][:, n, 0:GC],
                                     lambda p: qT[g % 2][p][:, tile * P:(tile + 1) * P],
                                     lambda p: k_diag[:, g, p, :], True, True)
                    mm.then_inc(scores_full, 1)

                def value_product(b, g, n, bank, probs_split):
                    pe.wait_ge(t_split, probs_split)
                    if isinstance(b, int) and b == 0:
                        pe.wait_ge(first_values_loaded, 16 * PIECES * G)
                    else:
                        pe.wait_ge(values_loaded[g], 16 * PIECES * b)
                    pe.wait_ge(m_split, n - 2)
                    for c in range(NC):
                        mm = matmul3(pe, m_bank[bank][:, :], lambda p: v_diag[:, g, p, c, :],
                                     lambda p: probsT[p][:, g % 2 * (NC - 1) + c, :], c == 0, c == NC - 1)
                    mm.then_inc(m_full, 1)

                def block_output(parity, tile, n, bank):
                    pe.wait_ge(m_split, n - 2)
                    for g in range(G):
                        mm = matmul3(pe, m_bank[bank][:, :], lambda p: oT[parity][p][:, g, tile * P:(tile + 1) * P],
                                     lambda p: woT[p][:, g, :], g == 0, g == G - 1)
                    mm.then_inc(m_full, 1)

                def turn(b, parity, place):
                    last_heads = None
                    for g, s in enumerate(slots_of(b, place)):
                        if s.finish:
                            for c in s.chunks[:2]:
                                transpose_probs(*s.back, c, *s.probs[c])
                        if s.score:
                            for half in range(2):
                                scores(b, g, half, s.queries_done, place == FIRST)
                        if s.finish and place != AFTER:
                            for c in s.chunks[2:]:
                                transpose_probs(*s.back, c, *s.probs[c])
                        if s.values_first:
                            value_product(*s.back, *s.values[:2], s.probs[s.chunks[-1]][0])
                            last_heads = s.values[0]
                        if s.queries:
                            if g == 3:
                                pe.wait_ge(t_split, x_split)
                            queries(parity ^ (g == 3), (g + 1) % G, *s.queries[:2])
                        if s.output:
                            if g == 2:
                                pe.wait_ge(m_split, last_heads)
                            block_output(parity ^ (g >= 2), s.output[1], *s.output[2:])
                        if s.x:
                            for i in range(2):
                                transpose_x(2 * (g - 1) + i, *s.x[i], b + 1)
                            x_split = s.x[1][0]
                        if s.finish and place == AFTER:
                            for c in s.chunks[2:]:
                                transpose_probs(*s.back, c, *s.probs[c])
                        if s.finish and not s.values_first:
                            value_product(*s.back, *s.values[:2], s.probs[s.chunks[-1]][0])
                            last_heads = s.values[0]
                    if place == AFTER:
                        pe.wait_ge(m_split, last_heads)

                over_batches(pe, turn)
                for tile, n, bank in outputs_after():
                    block_output((B - 1) % 2, tile, n, bank)

            @block.scalar
            def _(act):
                def bank_hi(dst, n, bank):
                    act.wait_ge(t_full, n)
                    act.activation(dst, t_bank[bank][:, :], ACT.Copy).then_inc(t_hi, 1)

                def exponentials(unit, half):
                    act.wait_ge(bias_ready, unit)
                    if not (isinstance(unit, int) and unit <= 2):
                        act.wait_ge(probs_ready, unit - 2)
                    for i in range(UR):
                        n, h = i // HG, i % HG
                        e = act.activation(exps[half][:, n, h * M:(h + 1) * M], pair_bank[half][:, n, h * M:(h + 1) * M],
                                           ACT.Exp, bias=exp_bias[half][:, i:i + 1], scale=SCALE,
                                           accum_out=exp_sum[half][:, i:i + 1])
                    e.then_inc(exps_ready, 1)

                def queries_hi(q, n, bank):
                    act.wait_ge(m_full, n)
                    act.activation(qT[q % 2][0][:, :], m_bank[bank][:, :], ACT.Identity,
                                   bias=bq_col[:, q:q + 1]).then_inc(m_hi, 1)

                def turn(b, parity, place):
                    for g, s in enumerate(slots_of(b, place)):
                        if s.finish:
                            for c in s.chunks:
                                bank_hi(probsT[0][:, c, :], *s.probs[c])
                        if s.score:
                            exponentials(2 * G * b + 2 * g + 1, 0)
                        if s.queries:
                            queries_hi((g + 1) % G, *s.queries[:2])
                        if s.score:
                            exponentials(2 * G * b + 2 * g + 2, 1)
                        if s.x:
                            for i in range(2):
                                bank_hi(xT[1 - parity][0][:, 2 * (g - 1) + i, :], *s.x[i])
                        if s.finish:
                            n, bank, _ = s.values
                            act.wait_ge(m_full, n)
                            act.activation(oT[parity ^ (g < 2)][0][:, s.back[1], :], m_bank[bank][:, :], ACT.Copy)\
                               .then_inc(m_hi, 1)

                over_batches(act, turn)

            @block.vector
            def _(dve):
                def bank_lo(dst, hi, n, bank):
                    dve.wait_ge(t_hi, n)
                    dve.tensor_tensor(dst, t_bank[bank][:, :], hi.bitcast(F32), ALU.subtract).then_inc(t_split, 1)

                def probs_lo(c, n, bank):
                    bank_lo(probsT[1][:, c, :], probsT[0][:, c, :], n, bank)

                def peaks(unit, half):
                    dve.wait_ge(scores_full, unit)
                    dve.tensor_reduce(peak[half][:, :].rearrange("p (n h) -> p n h", h=HG), scores_view(half),
                                      AX_X, ALU.max).then_inc(peak_ready, 1)
                    dve.wait_ge(peak_ready, unit)
                    dve.tensor_scalar(exp_bias[half][:, :], peak[half][:, :], -SCALE, None, ALU.mult)\
                       .then_inc(bias_ready, 1)

                def inverse(unit, half):
                    dve.wait_ge(exps_ready, unit)
                    dve.reciprocal(exp_inv[half][:, :], exp_sum[half][:, :]).then_inc(inv_ready, 1)

                def queries_lo(q, bank, h):
                    dve.wait_ge(m_hi, h)
                    dve.scalar_tensor_tensor(out=qT[q % 2][1][:, :], in0=m_bank[bank][:, :], scalar=bq_col[:, q:q + 1],
                                             in1=qT[q % 2][0][:, :].bitcast(F32), op0=ALU.add, op1=ALU.subtract)\
                       .then_inc(m_split, 1)

                def heads_lo(parity, g, bank, h):
                    dve.wait_ge(m_hi, h)
                    dve.tensor_tensor(oT[parity][1][:, g, :], m_bank[bank][:, :], oT[parity][0][:, g, :].bitcast(F32),
                                      ALU.subtract).then_inc(m_split, 1)

                def gate_output(b, tile, n, bank):
                    dve.wait_ge(m_full, n)
                    dve.wait_ge(residual_ready, NT * b + tile + 1)
                    dve.scalar_tensor_tensor(out=residual[tile][:, :], in0=m_bank[bank][:, :], scalar=tanh_g[:, 0:1],
                                             in1=residual[tile][:, :], op0=ALU.mult, op1=ALU.add).then_inc(m_split, 1)

                def turn(b, parity, place):
                    for g, s in enumerate(slots_of(b, place)):
                        unit = 2 * G * b + 2 * g
                        if s.finish:
                            for c in s.chunks[:2]:
                                probs_lo(c, *s.probs[c])
                        if s.score:
                            peaks(unit + 1, 0)
                            peaks(unit + 2, 1)
                        if s.finish:
                            for c in s.chunks[2:]:
                                probs_lo(c, *s.probs[c])
                        if g == 0 and place != AFTER:
                            sums(dve, b + 2, range(NT // 2))
                        if g == 1 and place != AFTER:
                            normalise(dve, b + 2)
                        if s.score:
                            inverse(unit + 1, 0)
                        if s.queries:
                            queries_lo((g + 1) % G, *s.queries[1:])
                        if g == 0 and place != AFTER:
                            sums(dve, b + 2, range(NT // 2, NT))
                            statistics(dve, b + 2)
                        if s.values_first:
                            heads_lo(parity ^ (g < 2), s.back[1], *s.values[1:])
                        if s.output:
                            gate_output(*s.output)
                        if s.score:
                            inverse(unit + 2, 1)
                        if s.x:
                            for i in range(2):
                                kt = 2 * (g - 1) + i
                                bank_lo(xT[1 - parity][1][:, kt, :], xT[1 - parity][0][:, kt, :], *s.x[i])
                        if s.finish and not s.values_first:
                            heads_lo(parity ^ (g < 2), s.back[1], *s.values[1:])

                over_batches(dve, turn)
                for tile, n, bank in outputs_after():
                    gate_output(B - 1, tile, n, bank)

        def ffn(st):
            AHEAD = 2
            LN_AT, NORM_AT = 3, 6
            XT_AT = {9: (0, 1), 10: (2, 3)}
            w1_split = [sb(st, f"w1_split{i}", [P, KT, F], F32R) for i in range(2)]
            w2_split = [sb(st, f"w2_split{i}", [P, FT, D], F32R) for i in range(2)]
            b2_rows = sb(st, "b2_rows", [P, D])
            hidden = [sb(st, f"hidden{i}", [P, N]) for i in range(2)]
            turns = sb(st, "turns", [P, N])
            sine = sb(st, "sine", [P, N])
            relu = [[sb(st, f"relu{s}_{i}", [P, N], F32R) for i in range(2)] for s in range(2)]

            b2_loaded = sem(st, "b2_loaded")
            b2_gated = sem(st, "b2_gated")
            chunk_hi = sem(st, "chunk_hi")
            chunk_split = sem(st, "chunk_split")
            t_full = sem(st, "t_full_f")
            t_hi = sem(st, "t_hi_f")
            t_split = sem(st, "t_split_f")
            h_full = sem(st, "h_full")
            h_ready = sem(st, "h_ready")
            whole_ready = sem(st, "whole_ready")
            part_ready = sem(st, "part_ready")
            sine_ready = sem(st, "sine_ready")
            mixed = sem(st, "mixed")
            relu_hi = sem(st, "relu_hi")
            relu_split = sem(st, "relu_split")
            relu_used = sem(st, "relu_used")
            y_full = sem(st, "y_full")
            y_ready = sem(st, "y_ready")
            residual_loaded = [sem(st, f"residual_loaded1_{t}") for t in range(NT)]
            residual_ready = sem(st, "residual_ready1")
            y_stored = [sem(st, f"y_stored1_{t}") for t in range(NT)]

            block = st.enter_context(nc.Block())

            def over_batches(eng, batch):
                batch(0, 0, False)
                with eng.Fori(1, B - 2, 2) as b:
                    batch(b, 1, False)
                    batch(b + 1, 0, False)
                batch(B - 1, 1, True)

            def chunk_parts(n):
                raw = w_chunk[n % STAGED]
                if n in w1_number:
                    g = w1_number.index(n)
                    return (raw[:, :].rearrange("p (k f) -> p k f", k=KT),
                            *(w1_split[i][:, :, HT * P * g:HT * P * (g + 1)] for i in range(2)))
                g = w2_number.index(n)
                return (raw[:, :].rearrange("p (f d) -> p f d", f=HT),
                        *(w2_split[i][:, HT * g:HT * (g + 1), :] for i in range(2)))

            def chunk_at(b, f):
                return f + STAGED - 1 if isinstance(b, int) and b == 0 and 1 <= f <= CHUNKS - STAGED else None

            @block.sync
            def _(sp):
                def load_residual(b, tile):
                    sp.dma_start(residual[tile][:, :], x1_tiles[b, :, tile]).then_inc(residual_loaded[tile], 16)

                def load_x(b):
                    sp.wait_ge(t_full, KT * (b - 1))
                    sp.dma_start(x_in[:, :, :], x1_tiles[b]).then_inc(x_loaded, 16)

                def store_y(b, tile):
                    sp.wait_ge(y_ready, NT * (b + 1) + tile + 1)
                    sp.dma_start(out_rows[NT * b + tile], residual[tile][:, :]).then_inc(y_stored[tile], 16)

                def outputs(b, last):
                    for tile in range(NT):
                        store_y(b, tile)
                    if not last:
                        for tile in range(NT):
                            sp.wait_ge(y_stored[tile], 16 * (b + 1))
                            load_residual(b + 1, tile)

                sp.dma_start(b2_rows[:, :], b2.rearrange("(a d) -> a d", a=1).to_broadcast([P, D])).then_inc(b2_loaded, 16)
                for tile in range(NT):
                    sp.wait_ge(x1_stored[tile], 16 * B)
                    load_residual(0, tile)
                for n in range(STAGED, CHUNKS):
                    sp.wait_ge(chunk_split, n - STAGED + 1)
                    load_chunk(sp, n)
                with sp.Fori(0, B - 2) as b:
                    load_x(b + 2)
                    outputs(b, False)
                outputs(B - 2, False)
                outputs(B - 1, True)
                for tile in range(NT):
                    sp.wait_ge(y_stored[tile], 16 * B)

            @block.gpsimd
            def _(pool):
                def batch(b, slot, last):
                    if not last:
                        rstd_of(pool, B + b + 2)
                    for tile in range(NT):
                        pool.wait_ge(residual_loaded[tile], 16 * (b + 1))
                        pool.tensor_tensor(residual[tile][:, :], residual[tile][:, :], b2_rows[:, :], ALU.add)\
                            .then_inc(residual_ready, 1)

                pool.wait_ge(b2_loaded, 16)
                pool.tensor_scalar(b2_rows[:, :], b2_rows[:, :], tanh_g[:, 1:2], 0.0, ALU.mult, ALU.add)\
                    .then_inc(b2_gated, 1)
                pool.wait_ge(b2_gated, 1)
                over_batches(pool, batch)

            @block.tensor
            def _(pe):
                def transpose_x(b, kts):
                    pe.wait_ge(normed, NT * (B + b + 1))
                    for kt in kts:
                        if not (isinstance(b, int) and b == 1 and kt < 2):
                            pe.wait_ge(t_split, KT * (b - 1) + kt - 1)
                        for tile in range(NT):
                            tr = pe.transpose(t_bank[kt % 2][:, tile * P:(tile + 1) * P],
                                              x_in[:, tile, kt * P:(kt + 1) * P], ident[:, :])
                        tr.then_inc(t_full, 1)

                def first_product(b, slot, f):
                    if isinstance(b, int) and b == 0:
                        if f % HT == 0:
                            pe.wait_ge(chunk_split, w1_number[f // HT] + 1)
                    elif f == 0:
                        pe.wait_ge(t_split, KT * b)
                    if not (isinstance(b, int) and b == 0 and f < 2):
                        pe.wait_ge(h_ready, FT * b + f - 1)
                    for kt in range(KT):
                        mm = matmul3(pe, m_bank[f % 2][:, :], lambda p: w1_split[p][:, kt, f * P:(f + 1) * P],
                                     lambda p: xT[slot][p][:, kt, :], kt == 0, kt == KT - 1)
                    mm.then_inc(h_full, 1)

                def second_product(b, f):
                    if isinstance(b, int) and b == 0 and f % HT == 0:
                        pe.wait_ge(chunk_split, w2_number[f // HT] + 1)
                    pe.wait_ge(relu_split, FT * b + f + 1)
                    for tile in range(NT):
                        if f == 0:
                            pe.wait_ge(y_ready, NT * b + tile + 1)
                        mm = matmul3(pe, pair_bank[tile // 2][:, tile % 2, :],
                                     lambda p: relu[f % 2][p][:, tile * P:(tile + 1) * P],
                                     lambda p: w2_split[p][:, f, :], f == 0, f == FT - 1)
                        if f == FT - 1:
                            mm.then_inc(y_full, 1)
                    if f < FT - 1:
                        mm.then_inc(relu_used, 1)

                def batch(b, slot, last):
                    for f in range(FT):
                        ahead = f + AHEAD
                        if ahead < FT:
                            first_product(b, slot, ahead)
                        elif not last:
                            first_product(b + 1, 1 - slot, ahead - FT)
                        second_product(b, f)
                        if f in XT_AT and not last:
                            transpose_x(b + 1, XT_AT[f])

                for f in range(AHEAD):
                    first_product(0, 0, f)
                over_batches(pe, batch)

            @block.scalar
            def _(act):
                def x_hi(b, slot, kts):
                    for kt in kts:
                        act.wait_ge(t_full, KT * (b - 1) + kt + 1)
                        act.activation(xT[slot][0][:, kt, :], t_bank[kt % 2][:, :], ACT.Copy).then_inc(t_hi, 1)

                def weight_hi(n):
                    raw, hi, _ = chunk_parts(n)
                    act.wait_ge(chunk_loaded[n % STAGED], 16 * (n // STAGED + 1))
                    act.activation(hi, raw, ACT.Copy).then_inc(chunk_hi, 1)

                def relu_of(b, f):
                    act.wait_ge(mixed, FT * b + f + 1)
                    act.activation(relu[f % 2][0][:, :], hidden[f % 2][:, :], ACT.Relu).then_inc(relu_hi, 1)

                def step(b, f):
                    act.wait_ge(h_full, FT * b + f + 1)
                    if f:
                        relu_of(b, f - 1)
                    act.activation(hidden[f % 2][:, :], m_bank[f % 2][:, :], ACT.Identity,
                                   bias=b1_col[:, f % FT:f % FT + 1])
                    act.activation(turns[:, :], m_bank[f % 2][:, :], ACT.Identity, scale=0.1 / TWO_PI,
                                   bias=turns_phase[:, f % FT:f % FT + 1]).then_inc(h_ready, 1)
                    if chunk_at(b, f) is not None:
                        weight_hi(chunk_at(b, f))
                    act.wait_ge(part_ready, FT * b + f + 1)
                    act.activation(sine[:, :], turns[:, :], ACT.Sin, scale=TWO_PI_BELOW).then_inc(sine_ready, 1)

                def batch(b, slot, last):
                    for f in range(1, FT):
                        step(b, f)
                        if f - AHEAD in XT_AT and not last:
                            x_hi(b + 1, 1 - slot, XT_AT[f - AHEAD])
                    if last:
                        act.wait_ge(relu_used, (FT - 1) * b + FT - 2)
                        relu_of(b, FT - 1)
                    else:
                        step(b, FT)

                for n in range(STAGED):
                    weight_hi(n)
                step(0, 0)
                over_batches(act, batch)

            @block.vector
            def _(dve):
                def weight_lo(n):
                    raw, hi, lo = chunk_parts(n)
                    dve.wait_ge(chunk_hi, n + 1)
                    dve.tensor_tensor(lo, raw, hi.bitcast(F32), ALU.subtract).then_inc(chunk_split, 1)

                def x_lo(b, slot, kts):
                    for kt in kts:
                        dve.wait_ge(t_hi, KT * (b - 1) + kt + 1)
                        dve.tensor_tensor(xT[slot][1][:, kt, :], t_bank[kt % 2][:, :],
                                          xT[slot][0][:, kt, :].bitcast(F32), ALU.subtract).then_inc(t_split, 1)

                def relu_lo(b, f):
                    dve.wait_ge(relu_hi, FT * b + f + 1)
                    dve.scalar_tensor_tensor(out=relu[f % 2][1][:, :], in0=hidden[f % 2][:, :], scalar=0.0,
                                             in1=relu[f % 2][0][:, :].bitcast(F32), op0=ALU.max, op1=ALU.subtract)\
                       .then_inc(relu_split, 1)

                def step(b, f):
                    if f:
                        relu_lo(b, f - 1)
                    n = FT * b + f + 1
                    dve.wait_ge(h_ready, n)
                    dve.tensor_scalar(sine[:, :], turns[:, :], ROUND_MAGIC, ROUND_MAGIC, ALU.add, ALU.subtract)\
                       .then_inc(whole_ready, 1)
                    dve.wait_ge(whole_ready, n)
                    dve.tensor_tensor(turns[:, :], turns[:, :], sine[:, :], ALU.subtract).then_inc(part_ready, 1)
                    if chunk_at(b, f) is not None:
                        weight_lo(chunk_at(b, f))
                    dve.wait_ge(sine_ready, n)
                    dve.scalar_tensor_tensor(out=hidden[f % 2][:, :], in0=sine[:, :],
                                             scalar=sine_gain[:, f % FT:f % FT + 1], in1=hidden[f % 2][:, :],
                                             op0=ALU.mult, op1=ALU.add).then_inc(mixed, 1)

                def outputs(b):
                    for tile in range(NT):
                        dve.wait_ge(y_full, NT * b + tile + 1)
                        dve.wait_ge(residual_ready, NT * b + tile + 1)
                        dve.scalar_tensor_tensor(out=residual[tile][:, :], in0=pair_bank[tile // 2][:, tile % 2, :],
                                                 scalar=tanh_g[:, 1:2], in1=residual[tile][:, :],
                                                 op0=ALU.mult, op1=ALU.add).then_inc(y_ready, 1)

                def batch(b, slot, last):
                    for f in range(1, FT):
                        step(b, f)
                        if not last:
                            if f == LN_AT:
                                sums(dve, B + b + 2)
                                statistics(dve, B + b + 2)
                            if f == NORM_AT:
                                normalise(dve, B + b + 2)
                            if f - AHEAD in XT_AT:
                                x_lo(b + 1, 1 - slot, XT_AT[f - AHEAD])
                    if last:
                        relu_lo(b, FT - 1)
                    else:
                        step(b, FT)
                    outputs(b)

                dve.memset(sine[:, :], 0.0).then_inc(y_ready, NT)
                for n in range(STAGED):
                    weight_lo(n)
                step(0, 0)
                over_batches(dve, batch)

        setup()
        with ExitStack() as st:
            attention(st)
        att.close()
        with ExitStack() as st:
            ffn(st)


_INS = ['x', 'ctx_1024', 'g_xattn', 'g_ffn', 'L0_xattn_Wq', 'L0_xattn_bq', 'L0_xattn_Wk', 'L0_xattn_bk',
        'L0_xattn_Wv', 'L0_xattn_bv', 'L0_xattn_Wo', 'L0_xattn_bo', 'L0_ffn_W1', 'L0_ffn_b1',
        'L0_ffn_quantum_phases', 'L0_ffn_quantum_weights_real', 'L0_ffn_quantum_weights_imag', 'L0_ffn_W2',
        'L0_ffn_b2']
_OUTS = [((16, 512, 512), 'float32')]


def kernel(**inputs):
    import numpy as _np
    import concourse.bacc as _bacc
    from concourse import mybir as _mybir
    from concourse.bass_utils import run_bass_kernel_spmd as _run

    nc = _bacc.Bacc("TRN2", target_bir_lowering=False, num_devices=1)
    arrays, args = {}, []
    for name in _INS:
        a = _np.ascontiguousarray(inputs[name])
        arrays[f"in_{name}_dram"] = a
        args.append(nc.dram_tensor(f"in_{name}_dram", a.shape, _mybir.dt.from_np(a.dtype), kind="ExternalInput").ap())
    for i, (shape, dtype) in enumerate(_OUTS):
        dt = _mybir.dt.from_np(_np.dtype(dtype))
        args.append(nc.dram_tensor(f"out_{i}_dram", shape, dt, kind="ExternalOutput").ap())
    gated_attention_ffn_kernel(nc, *args)
    r = _run(nc, [arrays], core_ids=[0])
    got = tuple(r.results[0][f"out_{i}_dram"] for i in range(len(_OUTS)))
    return got[0]
```
